# Optimizing a Trainium2 kernel written in Bass

```python
import numpy as np
import jax
import jax.numpy as jnp

def _softmax(x, axis=-1):
    return jax.nn.softmax(x, axis=axis)

def _gelu(x):
    return jax.nn.gelu(x, approximate=True)

def _silu(x):
    return jax.nn.silu(x)

def _sigmoid(x):
    return jax.nn.sigmoid(x)

def _layernorm(x, axis=-1, eps=1e-05):
    m = jnp.mean(x, axis=axis, keepdims=True)
    v = jnp.var(x, axis=axis, keepdims=True)
    return (x - m) / jnp.sqrt(v + eps)

def _scatter_add(tgt, idx, src, axis=0):
    return tgt.at[idx].add(src)

def _segment_sum(src, seg, n):
    return jax.ops.segment_sum(src, seg, n)
kernel_name = 'mk_sandwich_d1_jaxref_r8_a41854'

def setup_inputs(seed: int=0):
    np.random.seed(seed)
    _w = jnp.asarray

    def _L0_attn_setup():
        import jax, jax.numpy as jnp
        import numpy as np
        from jax import lax
        D_MODEL = 128
        STATE_DIM = 64
        BATCH = 4
        SEQ_LEN = 1024

        def _cayley_eigenvalues(a_params, n):
            half = n // 2
            a_full = jnp.zeros((n,), dtype=a_params.dtype)
            a_full = a_full.at[1:half + 1].set(a_params)
            a_full = a_full.at[half + 1:].set(-a_params[::-1][:n - half - 1])
            a_hat = jnp.fft.fft(a_full)
            omega = jnp.imag(a_hat)
            ones = jnp.ones_like(omega)
            num = lax.complex(ones, -omega)
            den = lax.complex(ones, omega)
            return num / den
        key = jax.random.key(seed)
        k1, k2, k3, k4 = jax.random.split(key, 4)
        u = jax.random.normal(k1, (BATCH, SEQ_LEN, D_MODEL), dtype=jnp.float32)
        a_params = jax.random.normal(k2, (STATE_DIM // 2,), dtype=jnp.float32) * 0.1
        B_w = jax.random.normal(k3, (STATE_DIM, D_MODEL), dtype=jnp.float32) / np.sqrt(D_MODEL)
        C_w = jax.random.normal(k4, (D_MODEL, STATE_DIM), dtype=jnp.float32) / np.sqrt(STATE_DIM)
        D = jnp.ones((D_MODEL,), dtype=jnp.float32)
        return {'u': u, 'a_params': a_params, 'B_w': B_w, 'C_w': C_w, 'D': D}
    _L0_attn_in = _L0_attn_setup()

    def _L0_ffn_setup():
        import jax, jax.numpy as jnp
        import numpy as np
        B, S, H = (2, 128, 128)
        E, F = (8, 512)
        GATE_TEMP = 0.1
        key = jax.random.key(seed)
        ks = jax.random.split(key, 6)
        s_h = 1.0 / np.sqrt(H)
        s_f = 1.0 / np.sqrt(F)
        return {'hidden_states': jax.random.normal(ks[0], (B, S, H), dtype=jnp.float32), 'w_router': jax.random.normal(ks[1], (H, E), dtype=jnp.float32) * s_h, 'w_gating': jax.random.normal(ks[2], (H, E), dtype=jnp.float32) * s_h, 'w_gate': jax.random.normal(ks[3], (E, H, F), dtype=jnp.float32) * s_h, 'w_up': jax.random.normal(ks[4], (E, H, F), dtype=jnp.float32) * s_h, 'w_down': jax.random.normal(ks[5], (E, F, H), dtype=jnp.float32) * s_f}
    _L0_ffn_in = _L0_ffn_setup()
    _d = {'L0_attn_u': _L0_attn_in['u'], 'L0_attn_a_params': _L0_attn_in['a_params'], 'L0_attn_B_w': _L0_attn_in['B_w'], 'L0_attn_C_w': _L0_attn_in['C_w'], 'L0_attn_D': _L0_attn_in['D'], 'L0_ffn_w_router': _L0_ffn_in['w_router'], 'L0_ffn_w_gating': _L0_ffn_in['w_gating'], 'L0_ffn_w_gate': _L0_ffn_in['w_gate'], 'L0_ffn_w_up': _L0_ffn_in['w_up'], 'L0_ffn_w_down': _L0_ffn_in['w_down']}
    _x0 = _d['L0_attn_u']
    _d['L0_attn_u'] = jax.random.normal(jax.random.fold_in(jax.random.key(seed), 1), (16, 512, 128), dtype=_x0.dtype)
    del _x0
    return _d

def reference(L0_attn_u, L0_attn_a_params, L0_attn_B_w, L0_attn_C_w, L0_attn_D, L0_ffn_w_router, L0_ffn_w_gating, L0_ffn_w_gate, L0_ffn_w_up, L0_ffn_w_down):

    def _L0_attn_ref(u, a_params, B_w, C_w, D):
        import jax, jax.numpy as jnp
        import numpy as np
        from jax import lax
        D_MODEL = 128
        STATE_DIM = 64
        BATCH = 4
        SEQ_LEN = 1024

        def _cayley_eigenvalues(a_params, n):
            half = n // 2
            a_full = jnp.zeros((n,), dtype=a_params.dtype)
            a_full = a_full.at[1:half + 1].set(a_params)
            a_full = a_full.at[half + 1:].set(-a_params[::-1][:n - half - 1])
            a_hat = jnp.fft.fft(a_full)
            omega = jnp.imag(a_hat)
            ones = jnp.ones_like(omega)
            num = lax.complex(ones, -omega)
            den = lax.complex(ones, omega)
            return num / den
        batch, seq_len, d = u.shape
        n = B_w.shape[0]
        Bu = jnp.einsum('btd,nd->btn', u, B_w)
        eig = _cayley_eigenvalues(a_params, n)
        t = jnp.arange(seq_len, dtype=jnp.float32)
        kernel = jnp.exp(t[:, None] * jnp.log(eig)[None, :])
        fft_len = 1
        while fft_len < 2 * seq_len:
            fft_len *= 2
        pad = fft_len - seq_len
        kernel_padded = jnp.pad(kernel, ((0, pad), (0, 0)))
        K_hat = jnp.fft.fft(kernel_padded, axis=0)
        Bu_padded = jnp.pad(Bu, ((0, 0), (0, pad), (0, 0))).astype(jnp.complex64)
        Bu_hat = jnp.fft.fft(Bu_padded, axis=1)
        h = jnp.fft.ifft(K_hat[None] * Bu_hat, axis=1).real[:, :seq_len, :]
        y = jnp.einsum('btn,dn->btd', h, C_w) + D * u
        return y

    def _L0_ffn_ref(hidden_states, w_router, w_gating, w_gate, w_up, w_down):
        import jax, jax.numpy as jnp
        import numpy as np
        B, S, H = (2, 128, 128)
        E, F = (8, 512)
        GATE_TEMP = 0.1
        x = hidden_states
        router_probs = jax.nn.softmax(jnp.einsum('bsh,he->bse', x, w_router), axis=-1)
        gate_weights = jax.nn.softmax(jnp.einsum('bsh,he->bse', x, w_gating) / GATE_TEMP, axis=-1)
        g = jnp.einsum('bsh,ehf->ebsf', x, w_gate)
        u = jnp.einsum('bsh,ehf->ebsf', x, w_up)
        h = jax.nn.silu(g) * u
        expert_out = jnp.einsum('ebsf,efh->ebsh', h, w_down)
        cw = router_probs * gate_weights
        cw = cw / (jnp.sum(cw, axis=-1, keepdims=True) + 1e-09)
        out = jnp.einsum('ebsh,bse->bsh', expert_out, cw)
        return out
    x = L0_attn_u
    x = x + _layernorm(_L0_attn_ref(_layernorm(x, axis=-1), L0_attn_a_params, L0_attn_B_w, L0_attn_C_w, L0_attn_D), axis=-1)
    x = x + _layernorm(_L0_ffn_ref(_layernorm(x, axis=-1), L0_ffn_w_router, L0_ffn_w_gating, L0_ffn_w_gate, L0_ffn_w_up, L0_ffn_w_down), axis=-1)
    return x

_drawn_inputs = setup_inputs


def setup_inputs(seed=0):
    import zlib

    import numpy as np

    out = dict(_drawn_inputs(seed))
    spreads = {'L0_attn_D': (1.0, 0.2)}
    factors = {}
    for name, (base, spread) in spreads.items():
        noise = np.random.default_rng([zlib.crc32(name.encode()), seed]).standard_normal(out[name].shape)
        drawn = base * np.exp(spread * noise) if base else spread * noise
        out[name] = jnp.asarray(drawn.astype(out[name].dtype))
    for name, factor in factors.items():
        out[name] = (out[name] * factor).astype(out[name].dtype)
    return out
```

```python
from contextlib import ExitStack

import numpy as np

import concourse.bass as bass
from concourse import mybir

P = 128
NCHUNK, SEQ, D = 16, 512, 128
NT = SEQ // P
NS = 64
E, F = 8, 512
NB = F // P
UNITS = E * NB
WCOLS = 3 * F
LAG = 3
RING = 4
GATE_SHARP = 10.0
LN_EPS = 1e-5
MIX_EPS = 1e-9
PROJ = P + D + 2 * E

POOL_LO = (1,)


def on_pool(k):
    return k % 4 in POOL_LO


N_POOL_LO = sum(on_pool(k) for k in range(UNITS))
N_DVE_LO = UNITS - N_POOL_LO


def lo_count(k):
    return sum(on_pool(j) == on_pool(k) for j in range(k + 1))


def build(nc, x_in, proj_in, a_in, sines_in, d_in, wgate_in, wup_in, wdown_in, out):
    f32, f32r = mybir.dt.float32, mybir.dt.float32r
    ALU, ACT, AX = mybir.AluOpType, mybir.ActivationFunctionType, mybir.AxisListType

    x_tok = x_in.rearrange("b (j p) d -> b p j d", p=P)
    out_tok = out.rearrange("b (j p) d -> b p j d", p=P)
    wdown_v = wdown_in.rearrange("e (b p) h -> e p b h", p=P)
    cw_dram = nc.dram_tensor("cw_scratch", [2, E * NT, P], f32, kind="Internal").ap()

    with ExitStack() as ctx:
        def sb(name, shape, dt=f32):
            return ctx.enter_context(nc.sbuf_tensor(name, shape, dt))

        def ps(name):
            return ctx.enter_context(nc.psum_tensor(name, [P, SEQ], f32))

        def sem(name):
            return ctx.enter_context(nc.semaphore(name))

        ident = sb("ident", [P, P])
        half = sb("half", [P, NT])
        pair_mean = sb("pair_mean", [P, NT, 2])
        sharp = sb("sharp", [P, NT, 2, E])
        proj = sb("proj", [P, PROJ])
        proj_hi, proj_lo = sb("proj_hi", [P, PROJ], f32r), sb("proj_lo", [P, PROJ], f32r)
        a_col, sines = sb("a_col", [NS // 2, 1]), sb("sines", [NS // 2, P])
        d_col = sb("d_col", [P, 1])
        ang = sb("ang", [P, 8])
        trig = sb("trig", [P, SEQ])
        stage = sb("stage", [P, 2, WCOLS])
        w_hi, w_lo = sb("w_hi", [P, E, WCOLS], f32r), sb("w_lo", [P, E, WCOLS], f32r)
        x_sb = sb("x_sb", [P, NT, D])
        stats, mv = sb("stats", [P, NT, 6]), sb("mv", [P, NT, 2])
        var_eps, rstd, shift = sb("var_eps", [P, NT]), sb("rstd", [P, NT]), sb("shift", [P, NT])
        xn = sb("xn", [P, NT, D])
        act_hi, act_lo = sb("act_hi", [P, SEQ], f32r), sb("act_lo", [P, SEQ], f32r)
        y_sb = sb("y_sb", [P, SEQ])
        v_sb, sum_sb = sb("v_sb", [P, SEQ]), sb("sum_sb", [P, SEQ])
        z_sb = sb("z_sb", [P, NT, D])
        x1 = sb("x1", [P, 2, NT, D])
        lg, e_neg, e_pos = (sb(n, [P, NT, 2, E]) for n in ("lg", "e_neg", "e_pos"))
        gmax, gsum = sb("gmax", [P, NT, 2]), sb("gsum", [P, NT, 2])
        pr, psum_, den = sb("pr", [P, NT, E]), sb("psum_", [P, NT]), sb("den", [P, NT])
        cw_pad = sb("cw_pad", [P, P])
        cw_t = sb("cw_t", [E * NT, P])
        xe_hi, xe_lo = sb("xe_hi", [P, 2, SEQ], f32r), sb("xe_lo", [P, 2, SEQ], f32r)
        gate = sb("gate", [P, 2, SEQ])
        hid = sb("hid", [P, RING, SEQ])
        hid_hi, hid_lo = sb("hid_hi", [P, RING, SEQ], f32r), sb("hid_lo", [P, RING, SEQ], f32r)
        cw_b = sb("cw_b", [P, 4, SEQ])
        y_part = sb("y_part", [P, 2, SEQ])
        acc = sb("acc", [P, 2, SEQ])
        stats2, mv2 = sb("stats2", [P, NT, 6]), sb("mv2", [P, NT, 2])
        var_eps2, rstd2, shift2 = sb("var_eps2", [P, NT]), sb("rstd2", [P, NT]), sb("shift2", [P, NT])
        o_sb = sb("o_sb", [P, NT, D])

        g_ps, u_ps = [ps("g0"), ps("g1")], [ps("u0"), ps("u1")]
        y_ps = [ps("y0"), ps("y1")]
        m_ps = ps("m_ps")
        n_ps = ps("n_ps")

        x_loaded, small_loaded, out_free = sem("x_loaded"), sem("small_loaded"), sem("out_free")
        w_loaded = [sem("w_loaded0"), sem("w_loaded1")]
        w_hi_done, w_lo_done = sem("w_hi_done"), sem("w_lo_done")
        const_ready = sem("const_ready")
        proj_split, omega_ready, trig_link, trig_ready = sem("proj_split"), sem("omega_ready"), sem("trig_link"), sem("trig_ready")
        cw_stored, cw_spread = sem("cw_stored"), [sem(f"cw_spread{i}") for i in range(4)]
        mix_link = sem("mix_link")
        var_ready, rstd_ready = sem("var_ready"), sem("rstd_ready")
        xn_ready, xn_turned = sem("xn_ready"), sem("xn_turned")
        act_hi_ready, act_lo_ready, du_ready = sem("act_hi_ready"), sem("act_lo_ready"), sem("du_ready")
        bu_ready, w_ready, mixed_ready, y_ready = sem("bu_ready"), sem("w_ready"), sem("mixed_ready"), sem("y_ready")
        y_turned, shift_ready, z_ready, x1_ready = sem("y_turned"), sem("shift_ready"), sem("z_ready"), sem("x1_ready")
        xe_turned, xe_hi_ready, xe_lo_ready = sem("xe_turned"), sem("xe_hi_ready"), sem("xe_lo_ready")
        logits_ready, lg_ready, silus_ready = sem("logits_ready"), sem("lg_ready"), sem("silus_ready")
        cw_ready, cw_turned, cw_t_ready = sem("cw_ready"), sem("cw_turned"), sem("cw_t_ready")
        gu_ready, gate_ready, hid_ready = sem("gu_ready"), sem("gate_ready"), sem("hid_ready")
        hi_ready, lo_dve, lo_pool = sem("hi_ready"), sem("lo_dve"), sem("lo_pool")
        down_done, part_ready, part_added = sem("down_done"), sem("part_ready"), sem("part_added")
        fin_link, fin_turned, fin_var, fin_rstd = sem("fin_link"), sem("fin_turned"), sem("fin_var"), sem("fin_rstd")
        fin_shift, fin_z, fin_ready = sem("fin_shift"), sem("fin_z"), sem("fin_ready")

        MIX_LINKS, FIN_LINKS, ADDS = 20, 3, E - 1

        def for_chunks(eng, body):
            body(0, 0, True, False)
            with eng.Fori(0, (NCHUNK - 2) // 2) as i:
                body(2 * i + 1, 1, False, False)
                body(2 * i + 2, 0, False, False)
            body(NCHUNK - 1, (NCHUNK - 1) % 2, False, True)

        block = ctx.enter_context(nc.Block())

        @block.sync
        def _(sp):
            def load_x(c):
                sp.dma_start(x_sb[:], x_tok[c]).then_inc(x_loaded, 16)

            def load_expert(e):
                if e >= 2:
                    sp.wait_ge(w_lo_done, e - 1)
                    sp.wait_ge(w_hi_done, e - 1)
                s = e % 2
                sp.dma_start(stage[:, s, 0:F], wgate_in[e]).then_inc(w_loaded[s], 16)
                sp.dma_start(stage[:, s, F:2 * F], wup_in[e]).then_inc(w_loaded[s], 16)
                sp.dma_start(stage[:, s, 2 * F:].rearrange("p (b h) -> p b h", b=NB),
                             wdown_v[e]).then_inc(w_loaded[s], 16)

            def store_cw(c, par):
                sp.wait_ge(cw_t_ready, c + 1)
                sp.dma_start(cw_dram[par], cw_t[:]).then_inc(cw_stored, 16)

            def spread_cw(c, par, e, first):
                if e == 0:
                    sp.wait_ge(cw_stored, 16 * (c + 1))
                if not (first and e < 4):
                    sp.wait_ge(part_ready, E * c + e - 3)
                row = cw_dram[par, e * NT:(e + 1) * NT, :].rearrange("j p -> (j p)")
                row = row.rearrange("(a t) -> a t", a=1).broadcast_to([P, SEQ])
                sp.dma_start(cw_b[:, e % 4, :], row).then_inc(cw_spread[e % 4], 16)

            def store_out(c):
                sp.wait_ge(fin_ready, c + 1)
                sp.dma_start(out_tok[c], o_sb[:]).then_inc(out_free, 16)

            load_x(0)
            sp.dma_start(proj[:], proj_in).then_inc(small_loaded, 16)
            sp.dma_start(a_col[:], a_in).then_inc(small_loaded, 16)
            sp.dma_start(sines[:], sines_in).then_inc(small_loaded, 16)
            sp.dma_start(d_col[:], d_in).then_inc(small_loaded, 16)
            load_expert(0)
            load_expert(1)

            def body(c, par, first, last):
                store_cw(c, par)
                if not last:
                    sp.wait_ge(x1_ready, c + 1)
                    load_x(c + 1)
                for e in range(E):
                    spread_cw(c, par, e, first)
                    if e == 4 and not first:
                        store_out(c - 1)
                    if first and e + 2 < E:
                        load_expert(e + 2)

            for_chunks(sp, body)
            store_out(NCHUNK - 1)
            sp.wait_ge(out_free, 16 * (NCHUNK + 1))
            sp.wait_ge(cw_stored, 16 * NCHUNK)

        @block.tensor
        def _(pe):
            def exact(dst, w_h, w_l, x_h, x_l, start=True, stop=True):
                nc.tensor.matmul(dst, w_h, x_h, start=start, stop=False)
                nc.tensor.matmul(dst, w_h, x_l, start=False, stop=False)
                return nc.tensor.matmul(dst, w_l, x_h, start=False, stop=stop)

            def turn(dst, src):
                for j in range(NT):
                    last = nc.tensor.transpose(dst[:, j * P:(j + 1) * P], src(j), ident[:])
                return last

            def mix_turn_x(c, prologue=False):
                pe.wait_ge(xn_ready, 2 * c + 1)
                if not prologue:
                    pe.wait_ge(cw_t_ready, c)
                turn(n_ps, lambda j: xn[:, j, :]).then_inc(xn_turned, 1)

            def mix_bu(c, first=False):
                if first:
                    pe.wait_ge(lg_ready, c)
                else:
                    pe.wait_ge(fin_z, c - 1)
                exact_bu(c)

            def exact_bu(c):
                pe.wait_ge(act_hi_ready, 2 * c + 1)
                pe.wait_ge(act_lo_ready, 2 * c + 1)
                exact(m_ps[:], proj_hi[:, 0:P], proj_lo[:, 0:P], act_hi[:], act_lo[:]).then_inc(bu_ready, 1)

            def mix_c(c):
                pe.wait_ge(act_hi_ready, 2 * c + 2)
                pe.wait_ge(act_lo_ready, 2 * c + 2)
                exact(m_ps[:], proj_hi[:, P:P + D], proj_lo[:, P:P + D], act_hi[:], act_lo[:]).then_inc(mixed_ready, 1)

            def mix_turn_y(c):
                pe.wait_ge(y_ready, c + 1)
                turn(n_ps, lambda j: y_sb[:, j * P:(j + 1) * P]).then_inc(y_turned, 1)

            def mix_turn_xe(c):
                pe.wait_ge(xn_ready, 2 * c + 2)
                turn(n_ps, lambda j: xn[:, j, :]).then_inc(xe_turned, 1)

            def mix_logits(c, par):
                pe.wait_ge(xe_hi_ready, c + 1)
                pe.wait_ge(xe_lo_ready, c + 1)
                for j in range(NT):
                    t = slice(j * P, (j + 1) * P)
                    last = exact(m_ps[:, 2 * E * j:2 * E * (j + 1)], xe_hi[:, par, t], xe_lo[:, par, t],
                                 proj_hi[:, P + D:], proj_lo[:, P + D:])
                last.then_inc(logits_ready, 1)

            def mix_turn_cw(c):
                pe.wait_ge(cw_ready, c + 1)
                nc.tensor.transpose(n_ps[:, 0:P], cw_pad[:], ident[:]).then_inc(cw_turned, 1)

            def turn_out(c, par, last=False):
                pe.wait_ge(part_added, ADDS * (c + 1))
                pe.wait_ge(lg_ready, c + 1 if last else c + 2)
                turn(m_ps, lambda j: acc[:, par, j * P:(j + 1) * P]).then_inc(fin_turned, 1)

            def gate_up(c, par, k, first):
                e, b, buf = k // NB, k % NB, k % 2
                if first and b == 0:
                    pe.wait_ge(w_lo_done, e + 1)
                    pe.wait_ge(w_hi_done, e + 1)
                if not (first and k < 2):
                    pe.wait_ge(hid_ready, UNITS * c + k - 1)
                for dst, off in ((g_ps[buf], 0), (u_ps[buf], F)):
                    cols = slice(off + b * P, off + (b + 1) * P)
                    last = exact(dst[:], w_hi[:, e, cols], w_lo[:, e, cols], xe_hi[:, par, :], xe_lo[:, par, :])
                last.then_inc(gu_ready, 1)

            def down(c, k, first):
                e, b = k // NB, k % NB
                pe.wait_ge(hi_ready, UNITS * c + k + 1)
                if on_pool(k):
                    pe.wait_ge(lo_pool, N_POOL_LO * c + lo_count(k))
                else:
                    pe.wait_ge(lo_dve, N_DVE_LO * c + lo_count(k))
                if b == 0 and not (first and e < 2):
                    pe.wait_ge(part_ready, E * c + e - 1)
                cols = slice(2 * F + b * D, 2 * F + (b + 1) * D)
                last = exact(y_ps[e % 2][:], w_hi[:, e, cols], w_lo[:, e, cols],
                             hid_hi[:, k % RING, :], hid_lo[:, k % RING, :], start=b == 0, stop=b == NB - 1)
                last.then_inc(down_done, 1)

            pe.wait_ge(small_loaded, 64)
            nc.tensor.matmul(m_ps[:, 0:1], sines[:], a_col[:], start=True, stop=True).then_inc(omega_ready, 1)
            pe.wait_ge(const_ready, 4)
            mix_turn_x(0, prologue=True)
            pe.wait_ge(proj_split, 2)
            pe.wait_ge(trig_ready, 1)
            exact_bu(0)
            mix_c(0)
            mix_turn_y(0)
            mix_turn_xe(0)
            mix_logits(0, 0)

            def body(c, par, first, last):
                for k in range(UNITS):
                    gate_up(c, par, k, first)
                    if k >= LAG:
                        down(c, k - LAG, first)
                    elif not first:
                        down(c - 1, k - LAG + UNITS, False)
                    if k == 0:
                        mix_turn_cw(c)
                    if not first and k == 5:
                        turn_out(c - 1, 1 - par)
                    if not last:
                        if k == 6:
                            mix_turn_x(c + 1)
                        if k == 10:
                            mix_bu(c + 1, first)
                        if k == 15:
                            mix_c(c + 1)
                        if k == 18:
                            mix_turn_y(c + 1)
                        if k == 25:
                            mix_turn_xe(c + 1)
                        if k == 28:
                            mix_logits(c + 1, 1 - par)

            for_chunks(pe, body)
            for k in range(UNITS - LAG, UNITS):
                down(NCHUNK - 1, k, False)
            turn_out(NCHUNK - 1, (NCHUNK - 1) % 2, last=True)

        @block.scalar
        def _(act):
            def split_expert(e):
                act.wait_ge(w_loaded[e % 2], 48 * (e // 2 + 1))
                nc.scalar.activation(w_hi[:, e, :], stage[:, e % 2, :], ACT.Copy).then_inc(w_hi_done, 1)

            def mix_hi_x(c):
                act.wait_ge(xn_turned, c + 1)
                nc.scalar.activation(act_hi[:], n_ps[:], ACT.Copy).then_inc(act_hi_ready, 1)

            def mix_du(c):
                nc.scalar.activation(y_sb[:], n_ps[:], ACT.Copy, scale=d_col[:]).then_inc(du_ready, 1)

            def mix_hi_w(c):
                act.wait_ge(w_ready, c + 1)
                nc.scalar.activation(act_hi[:], v_sb[:], ACT.Copy).then_inc(act_hi_ready, 1)

            def mix_z(c):
                act.wait_ge(shift_ready, c + 1)
                for j in range(NT):
                    last = nc.scalar.activation(z_sb[:, j, :], n_ps[:, j * P:(j + 1) * P], ACT.Identity,
                                                bias=shift[:, j:j + 1], scale=rstd[:, j:j + 1])
                last.then_inc(z_ready, 1)

            def mix_hi_xe(c, par):
                act.wait_ge(xe_turned, c + 1)
                nc.scalar.activation(xe_hi[:, par, :], n_ps[:], ACT.Copy).then_inc(xe_hi_ready, 1)

            def mix_silus(c):
                act.wait_ge(lg_ready, c + 1)
                nc.scalar.activation(e_neg[:], lg[:], ACT.Silu)
                nc.scalar.activation(e_pos[:], lg[:], ACT.Silu, scale=-1.0).then_inc(silus_ready, 1)

            def mix_cw_t(c, first):
                act.wait_ge(cw_turned, c + 1)
                if not first:
                    act.wait_ge(cw_stored, 16 * c)
                nc.scalar.activation(cw_t[:], n_ps[0:E * NT, 0:P], ACT.Copy).then_inc(cw_t_ready, 1)

            def fin_scale(c):
                act.wait_ge(fin_shift, c + 1)
                act.wait_ge(out_free, 16 * (c + 1))
                for j in range(NT):
                    last = nc.scalar.activation(o_sb[:, j, :], m_ps[:, j * P:(j + 1) * P], ACT.Identity,
                                                bias=shift2[:, j:j + 1], scale=rstd2[:, j:j + 1])
                last.then_inc(fin_z, 1)

            def silu(c, k, first):
                act.wait_ge(gu_ready, UNITS * c + k + 1)
                if not (first and k < 2):
                    act.wait_ge(hid_ready, UNITS * c + k - 1)
                nc.scalar.activation(gate[:, k % 2, :], g_ps[k % 2][:], ACT.Silu).then_inc(gate_ready, 1)

            def hid_high(c, k, first):
                act.wait_ge(hid_ready, UNITS * c + k + 1)
                if not (first and k < RING):
                    act.wait_ge(down_done, UNITS * c + k + 1 - RING)
                nc.scalar.activation(hid_hi[:, k % RING, :], hid[:, k % RING, :], ACT.Copy).then_inc(hi_ready, 1)

            act.wait_ge(small_loaded, 64)
            nc.scalar.activation(proj_hi[:], proj[:], ACT.Copy).then_inc(proj_split, 1)
            mix_hi_x(0)
            mix_du(0)
            split_expert(0)
            mix_hi_w(0)
            split_expert(1)
            mix_z(0)
            mix_hi_xe(0, 0)
            mix_silus(0)

            def body(c, par, first, last):
                for k in range(UNITS):
                    silu(c, k, first)
                    if k >= 1:
                        hid_high(c, k - 1, first)
                    elif not first:
                        hid_high(c - 1, UNITS - 1, False)
                    if first and k % NB == 1 and k // NB + 2 < E:
                        split_expert(k // NB + 2)
                    if k == 0:
                        mix_cw_t(c, first)
                    if not first and k == 7:
                        fin_scale(c - 1)
                    if not last:
                        if k == 6:
                            mix_hi_x(c + 1)
                            mix_du(c + 1)
                        if k == 12:
                            mix_hi_w(c + 1)
                        if k == 20:
                            mix_z(c + 1)
                        if k == 25:
                            mix_hi_xe(c + 1, 1 - par)
                        if k == 29:
                            mix_silus(c + 1)

            for_chunks(act, body)
            hid_high(NCHUNK - 1, UNITS - 1, False)
            fin_scale(NCHUNK - 1)

        @block.vector
        def _(dve):
            def mean_var(src, st, m, ve, link, at):
                for j in range(NT):
                    last = nc.vector.bn_stats(st[:, j, :], src(j))
                last.then_inc(link, 1)
                dve.wait_ge(link, at + 1)
                nc.vector.tensor_tensor(m[:], st[:, :, 1:3], st[:, :, 4:6], ALU.add)
                nc.vector.tensor_tensor(ve[:], st[:, :, 1], st[:, :, 4], ALU.subtract).then_inc(link, 1)
                dve.wait_ge(link, at + 2)
                nc.vector.tensor_tensor(m[:], m[:], pair_mean[:], ALU.mult)
                nc.vector.scalar_tensor_tensor(out=ve[:], in0=ve[:], scalar=0.25, in1=ve[:], op0=ALU.mult,
                                               op1=ALU.mult).then_inc(link, 1)
                dve.wait_ge(link, at + 3)
                return nc.vector.scalar_tensor_tensor(out=ve[:], in0=m[:, :, 1], scalar=LN_EPS, in1=ve[:],
                                                      op0=ALU.add, op1=ALU.add)

            def normalise(dst, src):
                for j in range(NT):
                    last = nc.vector.tensor_scalar(dst[:, j, :], src(j), mv[:, j, 0:1], rstd[:, j:j + 1],
                                                   ALU.subtract, ALU.mult)
                return last

            def shifts(dst, m, r):
                return nc.vector.scalar_tensor_tensor(out=dst[:], in0=m[:, :, 0], scalar=-1.0, in1=r[:],
                                                      op0=ALU.mult, op1=ALU.mult)

            def mix_stats_x(c):
                dve.wait_ge(x_loaded, 16 * (c + 1))
                mean_var(lambda j: x_sb[:, j, :], stats, mv, var_eps, mix_link, MIX_LINKS * c).then_inc(var_ready, 1)

            def mix_norm_x(c):
                dve.wait_ge(rstd_ready, 3 * c + 1)
                normalise(xn, lambda j: x_sb[:, j, :]).then_inc(xn_ready, 1)

            def mix_lo_x(c):
                dve.wait_ge(du_ready, c + 1)
                nc.vector.tensor_tensor(act_lo[:], n_ps[:], act_hi[:].bitcast(f32), ALU.subtract).then_inc(act_lo_ready, 1)

            def mix_enter(c):
                dve.wait_ge(bu_ready, c + 1)
                nc.vector.tensor_tensor(v_sb[:], m_ps[:], trig[:], ALU.mult).then_inc(mix_link, 1)

            def mix_scan(c):
                dve.wait_ge(mix_link, MIX_LINKS * c + 4)
                nc.vector.tensor_tensor_scan(sum_sb[:], v_sb[:], v_sb[:], 0.0, ALU.add, ALU.bypass).then_inc(mix_link, 1)

            def mix_leave(c):
                dve.wait_ge(mix_link, MIX_LINKS * c + 5)
                nc.vector.tensor_tensor(v_sb[:], sum_sb[:], trig[:], ALU.mult).then_inc(w_ready, 1)

            def mix_lo_w(c):
                dve.wait_ge(w_ready, c + 1)
                dve.wait_ge(act_hi_ready, 2 * c + 2)
                nc.vector.tensor_tensor(act_lo[:], v_sb[:], act_hi[:].bitcast(f32), ALU.subtract).then_inc(act_lo_ready, 1)

            def mix_y(c):
                dve.wait_ge(mixed_ready, c + 1)
                nc.vector.tensor_tensor(y_sb[:], m_ps[:], y_sb[:], ALU.add).then_inc(y_ready, 1)

            def mix_stats_y(c):
                dve.wait_ge(y_turned, c + 1)
                mean_var(lambda j: n_ps[:, j * P:(j + 1) * P], stats, mv, var_eps, mix_link,
                         MIX_LINKS * c + 5).then_inc(var_ready, 1)

            def mix_shift(c):
                dve.wait_ge(rstd_ready, 3 * c + 2)
                shifts(shift, mv, rstd).then_inc(shift_ready, 1)

            def mix_stats_x1(c, par):
                dve.wait_ge(x1_ready, c + 1)
                mean_var(lambda j: x1[:, par, j, :], stats, mv, var_eps, mix_link, MIX_LINKS * c + 8).then_inc(var_ready, 1)

            def mix_norm_x1(c, par):
                dve.wait_ge(rstd_ready, 3 * c + 3)
                normalise(xn, lambda j: x1[:, par, j, :]).then_inc(xn_ready, 1)

            def mix_lo_xe(c, par):
                dve.wait_ge(xe_hi_ready, c + 1)
                nc.vector.tensor_tensor(xe_lo[:, par, :], n_ps[:], xe_hi[:, par, :].bitcast(f32), ALU.subtract).then_inc(xe_lo_ready, 1)

            def groups(t):
                return t[:].rearrange("p j r e -> p (j r) e")

            def wide(t, n):
                return t.unsqueeze(2).broadcast_to([P, t.shape[1], n])

            def mix_softmax_in(c):
                at = MIX_LINKS * c
                dve.wait_ge(logits_ready, c + 1)
                raw = m_ps[:, 0:NT * 2 * E].rearrange("p (g e) -> p g e", e=E)
                nc.vector.tensor_reduce(out=gmax[:].rearrange("p j r -> p (j r)"), in_=raw, op=ALU.max, axis=AX.X).then_inc(mix_link, 1)
                dve.wait_ge(mix_link, at + 12)
                nc.vector.tensor_tensor(groups(lg), raw, wide(gmax[:].rearrange("p j r -> p (j r)"), E), ALU.subtract).then_inc(mix_link, 1)
                dve.wait_ge(mix_link, at + 13)
                nc.vector.tensor_tensor(lg[:], lg[:], sharp[:], ALU.mult).then_inc(mix_link, 1)
                dve.wait_ge(mix_link, at + 14)
                nc.vector.tensor_scalar(lg[:], lg[:], -1.0, None, ALU.add).then_inc(lg_ready, 1)

            def mix_softmax_out(c):
                at = MIX_LINKS * c
                dve.wait_ge(silus_ready, c + 1)
                nc.vector.reciprocal(e_pos[:], e_pos[:]).then_inc(mix_link, 1)
                dve.wait_ge(mix_link, at + 15)
                nc.vector.scalar_tensor_tensor(out=groups(lg), in0=groups(e_neg), scalar=-1.0, in1=groups(e_pos),
                                                         op0=ALU.mult, op1=ALU.mult).then_inc(mix_link, 1)
                dve.wait_ge(mix_link, at + 16)
                nc.vector.tensor_reduce(out=gsum[:].rearrange("p j r -> p (j r)"), in_=groups(lg), op=ALU.add, axis=AX.X)
                nc.vector.tensor_tensor(pr[:], lg[:, :, 0, :], lg[:, :, 1, :], ALU.mult).then_inc(mix_link, 1)
                dve.wait_ge(mix_link, at + 17)
                nc.vector.tensor_reduce(out=psum_[:], in_=pr[:], op=ALU.add, axis=AX.X)
                nc.vector.tensor_tensor(den[:], gsum[:, :, 0], gsum[:, :, 1], ALU.mult).then_inc(mix_link, 1)
                dve.wait_ge(mix_link, at + 18)
                nc.vector.scalar_tensor_tensor(out=den[:], in0=den[:], scalar=MIX_EPS, in1=psum_[:],
                                                         op0=ALU.mult, op1=ALU.add).then_inc(mix_link, 1)
                dve.wait_ge(mix_link, at + 19)
                nc.vector.reciprocal(den[:], den[:]).then_inc(mix_link, 1)
                dve.wait_ge(mix_link, at + 20)
                nc.vector.tensor_tensor(cw_pad[:, 0:E * NT].rearrange("p (e j) -> p j e", j=NT), pr[:],
                                        wide(den[:], E), ALU.mult).then_inc(cw_ready, 1)

            def fin_stats(c):
                dve.wait_ge(fin_turned, c + 1)
                mean_var(lambda j: m_ps[:, j * P:(j + 1) * P], stats2, mv2, var_eps2, fin_link,
                         FIN_LINKS * c).then_inc(fin_var, 1)

            def fin_shifts(c):
                dve.wait_ge(fin_rstd, c + 1)
                shifts(shift2, mv2, rstd2).then_inc(fin_shift, 1)

            def hidden(c, k, first):
                dve.wait_ge(gate_ready, UNITS * c + k + 1)
                if not (first and k < RING):
                    cc, kk = (c, k - RING) if k >= RING else (c - 1, k - RING + UNITS)
                    if on_pool(kk):
                        dve.wait_ge(lo_pool, N_POOL_LO * cc + lo_count(kk))
                    else:
                        dve.wait_ge(lo_dve, N_DVE_LO * cc + lo_count(kk))
                nc.vector.tensor_tensor(hid[:, k % RING, :], gate[:, k % 2, :], u_ps[k % 2][:], ALU.mult).then_inc(hid_ready, 1)

            def hid_low(c, k, first):
                if on_pool(k):
                    return
                dve.wait_ge(hi_ready, UNITS * c + k + 1)
                nc.vector.tensor_tensor(hid_lo[:, k % RING, :], hid[:, k % RING, :], hid_hi[:, k % RING, :].bitcast(f32),
                                        ALU.subtract).then_inc(lo_dve, 1)

            def weigh(c, par, e, first):
                dve.wait_ge(down_done, UNITS * c + NB * (e + 1))
                dve.wait_ge(cw_spread[e % 4], 16 * (2 * c + e // 4 + 1))
                if e > 0 and not (first and e < 3):
                    dve.wait_ge(part_added, ADDS * c + max(e - 2, 0))
                dst = acc[:, par, :] if e == 0 else y_part[:, e % 2, :]
                nc.vector.tensor_tensor(dst, y_ps[e % 2][:], cw_b[:, e % 4, :], ALU.mult).then_inc(part_ready, 1)

            links = [0]

            def then(ins):
                links[0] += 1
                ins.then_inc(trig_link, 1)
                dve.wait_ge(trig_link, links[0])

            w, w2, r, co, si, t0 = (ang[:, i:i + 1] for i in range(6))
            nc.vector.memset(half[:], -0.5).then_inc(out_free, 16)
            nc.vector.memset(pair_mean[:, :, 0], 0.5)
            nc.vector.memset(pair_mean[:, :, 1], 1.0 / D)
            nc.vector.memset(sharp[:, :, 0, :], 1.0)
            nc.vector.memset(sharp[:, :, 1, :], GATE_SHARP)
            nc.vector.memset(cw_pad[:], 0.0).then_inc(const_ready, 1)
            slope = sum_sb
            spare = z_sb[:].rearrange("p j d -> p (j d)")
            nc.vector.memset(trig[0:NS, 0:1], 1.0)
            nc.vector.memset(trig[NS:P, 0:1], 0.0)
            nc.vector.memset(slope[0:NS, 0:1], 0.0)
            nc.vector.memset(slope[NS:P, 0:1], 1.0)
            dve.wait_ge(const_ready, 2)
            mix_stats_x(0)
            dve.wait_ge(omega_ready, 1)
            then(nc.vector.tensor_copy(w, m_ps[:, 0:1]))
            then(nc.vector.tensor_tensor(w2, w, w, ALU.mult))
            then(nc.vector.tensor_scalar(r, w2, 1.0, None, ALU.add))
            then(nc.vector.reciprocal(r, r))
            then(nc.vector.tensor_scalar(co, w2, -1.0, 1.0, ALU.mult, ALU.add))
            then(nc.vector.tensor_tensor(co, co, r, ALU.mult))
            then(nc.vector.scalar_tensor_tensor(out=si, in0=w, scalar=-2.0, in1=r, op0=ALU.mult, op1=ALU.mult))
            mix_norm_x(0)
            n = 1
            while n < SEQ:
                old, new = slice(0, n), slice(n, 2 * n)
                nc.vector.tensor_scalar(v_sb[:, old], slope[:, old], si, None, ALU.mult)
                then(nc.vector.tensor_scalar(spare[:, old], trig[:, old], si, None, ALU.mult))
                nc.vector.scalar_tensor_tensor(out=trig[:, new], in0=trig[:, old], scalar=co, in1=v_sb[:, old],
                                               op0=ALU.mult, op1=ALU.add)
                nc.vector.scalar_tensor_tensor(out=slope[:, new], in0=slope[:, old], scalar=co, in1=spare[:, old],
                                               op0=ALU.mult, op1=ALU.subtract)
                then(nc.vector.tensor_tensor(w, si, si, ALU.mult))
                then(nc.vector.scalar_tensor_tensor(out=si, in0=si, scalar=2.0, in1=co, op0=ALU.mult, op1=ALU.mult))
                then(nc.vector.scalar_tensor_tensor(out=co, in0=co, scalar=co, in1=w, op0=ALU.mult, op1=ALU.subtract))
                n *= 2
            nc.vector.tensor_copy(w, si).then_inc(trig_ready, 1)
            dve.wait_ge(small_loaded, 64)
            dve.wait_ge(proj_split, 1)
            nc.vector.tensor_tensor(proj_lo[:], proj[:], proj_hi[:].bitcast(f32), ALU.subtract).then_inc(proj_split, 1)
            mix_lo_x(0)
            mix_enter(0)
            mix_scan(0)
            mix_leave(0)
            mix_lo_w(0)
            mix_y(0)
            mix_stats_y(0)
            mix_shift(0)
            mix_stats_x1(0, 0)
            mix_norm_x1(0, 0)
            mix_lo_xe(0, 0)
            mix_softmax_in(0)
            mix_softmax_out(0)

            def body(c, par, first, last):
                for k in range(UNITS):
                    hidden(c, k, first)
                    if k >= 1:
                        hid_low(c, k - 1, first)
                    elif not first:
                        hid_low(c - 1, UNITS - 1, False)
                    if k % NB == 2 and k >= 6:
                        weigh(c, par, (k - 6) // NB, first)
                    if k == 2 and not first:
                        weigh(c - 1, 1 - par, E - 1, False)
                    if k == 5 and not first:
                        fin_stats(c - 1)
                    if k == 6 and not first:
                        fin_shifts(c - 1)
                    if not last:
                        if k == 2:
                            mix_stats_x(c + 1)
                        if k == 3:
                            mix_norm_x(c + 1)
                        if k == 6:
                            mix_lo_x(c + 1)
                        if k == 10:
                            mix_enter(c + 1)
                            mix_scan(c + 1)
                        if k == 11:
                            mix_leave(c + 1)
                        if k == 12:
                            mix_lo_w(c + 1)
                        if k == 15:
                            mix_y(c + 1)
                        if k == 18:
                            mix_stats_y(c + 1)
                        if k == 19:
                            mix_shift(c + 1)
                        if k == 21:
                            mix_stats_x1(c + 1, 1 - par)
                        if k == 22:
                            mix_norm_x1(c + 1, 1 - par)
                        if k == 25:
                            mix_lo_xe(c + 1, 1 - par)
                        if k == 28:
                            mix_softmax_in(c + 1)
                        if k == 29:
                            mix_softmax_out(c + 1)

            for_chunks(dve, body)
            hid_low(NCHUNK - 1, UNITS - 1, False)
            weigh(NCHUNK - 1, (NCHUNK - 1) % 2, E - 1, False)
            fin_stats(NCHUNK - 1)
            fin_shifts(NCHUNK - 1)

        @block.gpsimd
        def _(pool):
            def split_expert(e):
                pool.wait_ge(w_hi_done, e + 1)
                nc.gpsimd.tensor_tensor(w_lo[:, e, :], stage[:, e % 2, :], w_hi[:, e, :].bitcast(f32),
                                        ALU.subtract).then_inc(w_lo_done, 1)

            def mix_rstd(c, n):
                pool.wait_ge(var_ready, 3 * c + n)
                nc.gpsimd.tensor_tensor(rstd[:], var_eps[:], half[:], ALU.pow).then_inc(rstd_ready, 1)

            def mix_residual(c, par):
                pool.wait_ge(z_ready, c + 1)
                nc.gpsimd.tensor_tensor(x1[:, par], x_sb[:], z_sb[:], ALU.add).then_inc(x1_ready, 1)

            def fin_rsqrt(c):
                pool.wait_ge(fin_var, c + 1)
                nc.gpsimd.tensor_tensor(rstd2[:], var_eps2[:], half[:], ALU.pow).then_inc(fin_rstd, 1)

            def fin_residual(c, par):
                pool.wait_ge(fin_z, c + 1)
                nc.gpsimd.tensor_tensor(o_sb[:], x1[:, par], o_sb[:], ALU.add).then_inc(fin_ready, 1)

            def hid_low(c, k, first):
                if not on_pool(k):
                    return
                pool.wait_ge(hi_ready, UNITS * c + k + 1)
                nc.gpsimd.tensor_tensor(hid_lo[:, k % RING, :], hid[:, k % RING, :], hid_hi[:, k % RING, :].bitcast(f32),
                                        ALU.subtract).then_inc(lo_pool, 1)

            def add_part(c, par, e):
                pool.wait_ge(part_ready, E * c + e + 1)
                if e > 1:
                    pool.wait_ge(part_added, ADDS * c + e - 1)
                nc.gpsimd.tensor_tensor(acc[:, par, :], acc[:, par, :], y_part[:, e % 2, :], ALU.add).then_inc(part_added, 1)

            nc.gpsimd.memset(ident[:], 0.0).then_inc(const_ready, 1)
            pool.wait_ge(const_ready, 2)
            nc.gpsimd.affine_select(out=ident[:], in_=ident[:], compare_op=ALU.not_equal, fill=1.0, base=0,
                                    pattern=[[-1, P]], channel_multiplier=1).then_inc(const_ready, 2)
            mix_rstd(0, 1)
            split_expert(0)
            mix_rstd(0, 2)
            mix_residual(0, 0)
            mix_rstd(0, 3)
            split_expert(1)

            def body(c, par, first, last):
                for k in range(UNITS):
                    if k >= 1:
                        hid_low(c, k - 1, first)
                    elif not first:
                        hid_low(c - 1, UNITS - 1, False)
                    if k % NB == 2 and k >= 10:
                        add_part(c, par, (k - 6) // NB)
                    if k == 2 and not first:
                        add_part(c - 1, 1 - par, E - 1)
                    if first and k % NB == 1 and k // NB + 2 < E:
                        split_expert(k // NB + 2)
                    if k == 5 and not first:
                        fin_rsqrt(c - 1)
                    if k == 7 and not first:
                        fin_residual(c - 1, 1 - par)
                    if not last:
                        if k == 2:
                            mix_rstd(c + 1, 1)
                        if k == 18:
                            mix_rstd(c + 1, 2)
                        if k == 20:
                            mix_residual(c + 1, 1 - par)
                        if k == 21:
                            mix_rstd(c + 1, 3)

            for_chunks(pool, body)
            hid_low(NCHUNK - 1, UNITS - 1, False)
            add_part(NCHUNK - 1, (NCHUNK - 1) % 2, E - 1)
            fin_rsqrt(NCHUNK - 1)
            fin_residual(NCHUNK - 1, (NCHUNK - 1) % 2)


def sine_rows():
    m = np.arange(NS)
    source = np.where(m <= NS // 2, m - 1, NS - m)
    sign = np.where(m <= NS // 2, 1.0, -1.0) * (m > 0)
    wave = -np.sin(2.0 * np.pi * ((m[:, None] * m[None, :]) % NS) / NS)
    rows = np.zeros((NS // 2, NS))
    for i in range(1, NS):
        rows[source[i]] += sign[i] * wave[i]
    return np.concatenate([rows, rows], axis=1).astype(np.float32)


def kernel(L0_attn_u, L0_attn_a_params, L0_attn_B_w, L0_attn_C_w, L0_attn_D, L0_ffn_w_router, L0_ffn_w_gating,
           L0_ffn_w_gate, L0_ffn_w_up, L0_ffn_w_down):
    import concourse.bacc as bacc
    from concourse.bass_utils import run_bass_kernel_spmd

    b_t, c_t = np.asarray(L0_attn_B_w).T, np.asarray(L0_attn_C_w).T
    arrays = {
        "x_in": L0_attn_u,
        "proj_in": np.concatenate([b_t, b_t, np.concatenate([c_t, c_t], axis=0), L0_ffn_w_router, L0_ffn_w_gating], axis=1),
        "a_in": np.asarray(L0_attn_a_params).reshape(NS // 2, 1),
        "sines_in": sine_rows(),
        "d_in": np.asarray(L0_attn_D).reshape(D, 1),
        "wgate_in": L0_ffn_w_gate,
        "wup_in": L0_ffn_w_up,
        "wdown_in": L0_ffn_w_down,
    }
    arrays = {n: np.ascontiguousarray(a) for n, a in arrays.items()}
    nc = bacc.Bacc("TRN2", target_bir_lowering=False, num_devices=1)
    args = [nc.dram_tensor(n, a.shape, mybir.dt.from_np(a.dtype), kind="ExternalInput").ap() for n, a in arrays.items()]
    args.append(nc.dram_tensor("x_out", (NCHUNK, SEQ, D), mybir.dt.float32, kind="ExternalOutput").ap())
    build(nc, *args)
    return run_bass_kernel_spmd(nc, [arrays], core_ids=[0]).results[0]["x_out"]
```

```python
from contextlib import ExitStack

import numpy as np

import concourse.bass as bass
from concourse import mybir

P = 128
NCHUNK, SEQ, D = 16, 512, 128
NT = SEQ // P
NS = 64
E, F = 8, 512
NB = F // P
UNITS = E * NB
WCOLS = 3 * F
LAG = 3
RING = 4
GATE_SHARP = 10.0
AHEAD = 4
PIECES = WCOLS // F
TENSOR_AT = {"turn_cw": 3, "turn_x": 5, "bu": 9, "turn_out": 10, "c": 15, "turn_y": 16, "turn_xe": 26, "logits":
             27}
SCALAR_AT = {"cw_t": 3, "hi_x": 7, "du": 7, "fin_a": 12, "fin_b": 12, "hi_w": 13, "z_a": 18, "z_b": 19, "hi_xe":
             26, "silus": 29}
VECTOR_AT = {"weights": 1, "stats_x": 1, "var_x": 2, "norm_x": 3, "lo_x": 7, "enter": 8, "scan": 9, "fin_stats":
             9, "leave": 10, "fin_var": 10, "fin_shift": 11, "lo_w": 14, "y": 15, "stats_y": 16, "var_y": 16,
             "shift": 18, "stats_x1": 22, "var_x1": 23, "norm_x1": 24, "lo_xe": 26, "softmax": 28, "exps": 30,
             "products": 30}
GPSIMD_AT = {"rstd_x": 3, "fin_rstd": 11, "fin_add": 13, "rstd_y": 16, "residual": 18, "rstd_x1": 22}
LN_EPS = 1e-5
MIX_EPS = 1e-9
PROJ = P + D + 2 * E

POOL_LO = (1, 3)


def on_pool(k):
    return k % 4 in POOL_LO


N_POOL_LO = sum(on_pool(k) for k in range(UNITS))
N_DVE_LO = UNITS - N_POOL_LO


def lo_count(k):
    return sum(on_pool(j) == on_pool(k) for j in range(k + 1))


def build(nc, x_in, proj_in, a_in, sines_in, d_in, wgate_in, wup_in, wdown_in, out):
    f32, f32r = mybir.dt.float32, mybir.dt.float32r
    ALU, ACT, AX = mybir.AluOpType, mybir.ActivationFunctionType, mybir.AxisListType

    x_tok = x_in.rearrange("b (j p) d -> b p j d", p=P)
    out_tok = out.rearrange("b (j p) d -> b p j d", p=P)
    wdown_v = wdown_in.rearrange("e (b p) h -> e p b h", p=P)
    cw_dram = nc.dram_tensor("cw_scratch", [2, E * NT, P], f32, kind="Internal").ap()

    with ExitStack() as ctx:
        def sb(name, shape, dt=f32):
            return ctx.enter_context(nc.sbuf_tensor(name, shape, dt))

        def ps(name):
            return ctx.enter_context(nc.psum_tensor(name, [P, SEQ], f32))

        def sem(name):
            return ctx.enter_context(nc.semaphore(name))

        ident = sb("ident", [P, P])
        half = sb("half", [P, NT])
        pair_mean = sb("pair_mean", [P, NT, 2])
        sharp = sb("sharp", [P, NT, 2, E])
        proj = sb("proj", [P, PROJ])
        proj_hi, proj_lo = sb("proj_hi", [P, P + D], f32r), sb("proj_lo", [P, P + D], f32r)
        router = sb("router", [P, 2, 2 * E], f32r)
        a_col, sines = sb("a_col", [NS // 2, 1]), sb("sines", [NS // 2, P])
        d_col = sb("d_col", [P, 1])
        ang = sb("ang", [P, 8])
        trig = sb("trig", [P, SEQ])
        stage = sb("stage", [P, 2, WCOLS])
        w_hi, w_lo = sb("w_hi", [P, E, WCOLS], f32r), sb("w_lo", [P, E, WCOLS], f32r)
        x_sb = sb("x_sb", [P, NT, D])
        stats, mv = sb("stats", [P, NT, 6]), sb("mv", [P, NT, 2])
        var_eps, rstd, shift = sb("var_eps", [P, NT]), sb("rstd", [P, NT]), sb("shift", [P, NT])
        xn = sb("xn", [P, NT, D])
        act_hi, act_lo = sb("act_hi", [P, SEQ], f32r), sb("act_lo", [P, SEQ], f32r)
        y_sb = sb("y_sb", [P, SEQ])
        v_sb, sum_sb = sb("v_sb", [P, SEQ]), sb("sum_sb", [P, SEQ])
        z_sb = sb("z_sb", [P, NT, D])
        x1 = sb("x1", [P, 2, NT, D])
        lg, e_neg, e_pos = (sb(n, [P, NT, 2, E]) for n in ("lg", "e_neg", "e_pos"))
        gmax, gsum = sb("gmax", [P, NT, 2]), sb("gsum", [P, NT, 2])
        pr, psum_, den = sb("pr", [P, NT, E]), sb("psum_", [P, NT]), sb("den", [P, NT])
        cw_pad = sb("cw_pad", [P, P])
        cw_t = sb("cw_t", [E * NT, P])
        xe_hi, xe_lo = sb("xe_hi", [P, 2, SEQ], f32r), sb("xe_lo", [P, 2, SEQ], f32r)
        gate = sb("gate", [P, 2, SEQ])
        hid = sb("hid", [P, RING, SEQ])
        hid_hi, hid_lo = sb("hid_hi", [P, RING, SEQ], f32r), sb("hid_lo", [P, RING, SEQ], f32r)
        cw_b = sb("cw_b", [P, 4, SEQ])
        y_part = sb("y_part", [P, 2, SEQ])
        acc = sb("acc", [P, 2, SEQ])
        stats2, mv2 = sb("stats2", [P, NT, 6]), sb("mv2", [P, NT, 2])
        var_eps2, rstd2, shift2 = sb("var_eps2", [P, NT]), sb("rstd2", [P, NT]), sb("shift2", [P, NT])
        o_sb = sb("o_sb", [P, NT, D])

        g_ps, u_ps = [ps("g0"), ps("g1")], [ps("u0"), ps("u1")]
        y_ps = [ps("y0"), ps("y1")]
        m_ps = ps("m_ps")
        n_ps = ps("n_ps")

        angle_loaded, x_loaded, small_loaded, out_free = sem("angle_loaded"), sem("x_loaded"), sem("small_loaded"), sem("out_free")
        w_loaded = [sem("w_loaded0"), sem("w_loaded1")]
        w_hi_done, w_lo_done = sem("w_hi_done"), sem("w_lo_done")
        const_ready = sem("const_ready")
        proj_split, omega_ready, trig_link, trig_ready = sem("proj_split"), sem("omega_ready"), sem("trig_link"), sem("trig_ready")
        cw_stored, cw_spread = sem("cw_stored"), [sem(f"cw_spread{i}") for i in range(4)]
        mix_link = sem("mix_link")
        soft_link = sem("soft_link")
        var_ready, rstd_ready = sem("var_ready"), sem("rstd_ready")
        xn_ready, xn_turned = sem("xn_ready"), sem("xn_turned")
        act_hi_ready, act_lo_ready, du_ready = sem("act_hi_ready"), sem("act_lo_ready"), sem("du_ready")
        bu_ready, w_ready, mixed_ready, y_ready = sem("bu_ready"), sem("w_ready"), sem("mixed_ready"), sem("y_ready")
        y_turned, shift_ready, z_ready, x1_ready = sem("y_turned"), sem("shift_ready"), sem("z_ready"), sem("x1_ready")
        xe_turned, xe_hi_ready, xe_lo_ready = sem("xe_turned"), sem("xe_hi_ready"), sem("xe_lo_ready")
        logits_ready, raw_read, lg_ready, silus_ready = sem("logits_ready"), sem("raw_read"), sem("lg_ready"), sem("silus_ready")
        cw_ready, cw_turned, cw_t_ready = sem("cw_ready"), sem("cw_turned"), sem("cw_t_ready")
        gu_ready, gate_ready, hid_ready = sem("gu_ready"), sem("gate_ready"), sem("hid_ready")
        hi_ready, lo_dve, lo_pool = sem("hi_ready"), sem("lo_dve"), sem("lo_pool")
        down_done, part_ready, part_added = sem("down_done"), sem("part_ready"), sem("part_added")
        fin_link, fin_turned, fin_var, fin_rstd = sem("fin_link"), sem("fin_turned"), sem("fin_var"), sem("fin_rstd")
        fin_shift, fin_z, fin_ready = sem("fin_shift"), sem("fin_z"), sem("fin_ready")

        MIX_LINKS, SOFT_LINKS, FIN_LINKS, ADDS = 11, 8, 3, E - 1

        def for_chunks(eng, body):
            body(0, 0, True, False)
            with eng.Fori(0, (NCHUNK - 2) // 2) as i:
                body(2 * i + 1, 1, False, False)
                body(2 * i + 2, 0, False, False)
            body(NCHUNK - 1, (NCHUNK - 1) % 2, False, True)

        block = ctx.enter_context(nc.Block())

        @block.sync
        def _(sp):
            def load_x(c):
                sp.dma_start(x_sb[:], x_tok[c]).then_inc(x_loaded, 16)

            def load_expert(e):
                if e >= 2:
                    sp.wait_ge(w_lo_done, PIECES * (e - 1))
                s = e % 2
                sp.dma_start(stage[:, s, 0:F], wgate_in[e]).then_inc(w_loaded[s], 16)
                sp.dma_start(stage[:, s, F:2 * F], wup_in[e]).then_inc(w_loaded[s], 16)
                sp.dma_start(stage[:, s, 2 * F:].rearrange("p (b h) -> p b h", b=NB),
                             wdown_v[e]).then_inc(w_loaded[s], 16)

            def store_cw(c, par):
                sp.wait_ge(cw_t_ready, c + 1)
                sp.dma_start(cw_dram[par], cw_t[:]).then_inc(cw_stored, 16)

            def spread_cw(c, par, e, first):
                if e == 0:
                    sp.wait_ge(cw_stored, 16 * (c + 1))
                if not (first and e < 4):
                    sp.wait_ge(part_ready, E * c + e - 3)
                row = cw_dram[par, e * NT:(e + 1) * NT, :].rearrange("j p -> (j p)")
                row = row.rearrange("(a t) -> a t", a=1).broadcast_to([P, SEQ])
                sp.dma_start(cw_b[:, e % 4, :], row).then_inc(cw_spread[e % 4], 16)

            def store_out(c):
                sp.wait_ge(fin_ready, c + 1)
                sp.dma_start(out_tok[c], o_sb[:]).then_inc(out_free, 16)

            sp.dma_start(a_col[:], a_in).then_inc(angle_loaded, 16)
            sp.dma_start(sines[:], sines_in).then_inc(angle_loaded, 16)
            load_x(0)
            sp.dma_start(proj[:], proj_in).then_inc(small_loaded, 16)
            sp.dma_start(d_col[:], d_in).then_inc(small_loaded, 16)
            for e in range(AHEAD + 2):
                load_expert(e)

            def body(c, par, first, last):
                if not last:
                    sp.wait_ge(x1_ready, c + 1)
                    load_x(c + 1)
                store_cw(c, par)
                for e in range(E):
                    spread_cw(c, par, e, first)
                    if e == 4 and not first:
                        store_out(c - 1)
                    if first and e + AHEAD + 2 < E:
                        load_expert(e + AHEAD + 2)

            for_chunks(sp, body)
            store_out(NCHUNK - 1)
            sp.wait_ge(out_free, 16 * (NCHUNK + 1))
            sp.wait_ge(cw_stored, 16 * NCHUNK)

        @block.tensor
        def _(pe):
            def exact(dst, w_h, w_l, x_h, x_l, start=True, stop=True):
                nc.tensor.matmul(dst, w_h, x_h, start=start, stop=False)
                nc.tensor.matmul(dst, w_h, x_l, start=False, stop=False)
                return nc.tensor.matmul(dst, w_l, x_h, start=False, stop=stop)

            def turn(dst, src):
                for j in range(NT):
                    last = nc.tensor.transpose(dst[:, j * P:(j + 1) * P], src(j), ident[:])
                return last

            def mix_turn_x(c, prologue=False):
                pe.wait_ge(xn_ready, 2 * c + 1)
                if not prologue:
                    pe.wait_ge(cw_t_ready, c)
                turn(n_ps, lambda j: xn[:, j, :]).then_inc(xn_turned, 1)

            def mix_bu(c, prologue=False):
                if prologue:
                    pe.wait_ge(trig_ready, 1)
                else:
                    pe.wait_ge(raw_read, c)
                pe.wait_ge(act_hi_ready, 2 * c + 1)
                pe.wait_ge(act_lo_ready, 2 * c + 1)
                exact(m_ps[:], proj_hi[:, 0:P], proj_lo[:, 0:P], act_hi[:], act_lo[:]).then_inc(bu_ready, 1)

            def mix_c(c):
                pe.wait_ge(act_hi_ready, 2 * c + 2)
                pe.wait_ge(act_lo_ready, 2 * c + 2)
                exact(m_ps[:], proj_hi[:, P:P + D], proj_lo[:, P:P + D], act_hi[:], act_lo[:]).then_inc(mixed_ready, 1)

            def mix_turn_y(c, first):
                pe.wait_ge(y_ready, c + 1)
                if not first:
                    pe.wait_ge(fin_z, c - 1)
                turn(n_ps, lambda j: y_sb[:, j * P:(j + 1) * P]).then_inc(y_turned, 1)

            def mix_turn_xe(c):
                pe.wait_ge(xn_ready, 2 * c + 2)
                turn(n_ps, lambda j: xn[:, j, :]).then_inc(xe_turned, 1)

            def mix_logits(c, par):
                pe.wait_ge(xe_hi_ready, c + 1)
                pe.wait_ge(xe_lo_ready, c + 1)
                for j in range(NT):
                    t, at = slice(j * P, (j + 1) * P), 4 * E * j
                    nc.tensor.matmul(m_ps[:, at:at + 4 * E], xe_hi[:, par, t], router[:], start=True, stop=False)
                    last = nc.tensor.matmul(m_ps[:, at:at + 2 * E], xe_lo[:, par, t], router[:, 0, :], start=False, stop=True)
                last.then_inc(logits_ready, 1)

            def mix_turn_cw(c):
                pe.wait_ge(cw_ready, c + 1)
                nc.tensor.transpose(n_ps[:, 0:P], cw_pad[:], ident[:]).then_inc(cw_turned, 1)

            def turn_out(c, par, tail=False, last=False):
                pe.wait_ge(part_added, ADDS * (c + 1))
                if last:
                    pe.wait_ge(fin_z, c)
                elif tail:
                    pe.wait_ge(cw_t_ready, c + 2)
                else:
                    pe.wait_ge(act_lo_ready, 2 * c + 5)
                turn(n_ps, lambda j: acc[:, par, j * P:(j + 1) * P]).then_inc(fin_turned, 1)

            def gate_up(c, par, k, first):
                e, b, buf = k // NB, k % NB, k % 2
                if first and b == 0:
                    pe.wait_ge(w_lo_done, PIECES * (e + 1))
                if not (first and k < 2):
                    pe.wait_ge(hid_ready, UNITS * c + k - 1)
                for dst, off in ((g_ps[buf], 0), (u_ps[buf], F)):
                    cols = slice(off + b * P, off + (b + 1) * P)
                    last = exact(dst[:], w_hi[:, e, cols], w_lo[:, e, cols], xe_hi[:, par, :], xe_lo[:, par, :])
                last.then_inc(gu_ready, 1)

            def down(c, k, first):
                e, b = k // NB, k % NB
                pe.wait_ge(hi_ready, UNITS * c + k + 1)
                if on_pool(k):
                    pe.wait_ge(lo_pool, N_POOL_LO * c + lo_count(k))
                else:
                    pe.wait_ge(lo_dve, N_DVE_LO * c + lo_count(k))
                if b == 0 and not (first and e < 2):
                    pe.wait_ge(part_ready, E * c + e - 1)
                cols = slice(2 * F + b * D, 2 * F + (b + 1) * D)
                last = exact(y_ps[e % 2][:], w_hi[:, e, cols], w_lo[:, e, cols],
                             hid_hi[:, k % RING, :], hid_lo[:, k % RING, :], start=b == 0, stop=b == NB - 1)
                last.then_inc(down_done, 1)

            pe.wait_ge(angle_loaded, 32)
            nc.tensor.matmul(m_ps[:, 0:1], sines[:], a_col[:], start=True, stop=True).then_inc(omega_ready, 1)
            pe.wait_ge(const_ready, 4)
            mix_turn_x(0, prologue=True)
            pe.wait_ge(proj_split, 2)
            mix_bu(0, prologue=True)
            mix_c(0)
            mix_turn_y(0, True)
            mix_turn_xe(0)
            pe.wait_ge(xe_hi_ready, 1)
            pe.wait_ge(xe_lo_ready, 1)

            def body(c, par, first, last):
                for k in range(UNITS):
                    gate_up(c, par, k, first)
                    if k >= LAG:
                        down(c, k - LAG, first)
                    elif not first:
                        down(c - 1, k - LAG + UNITS, False)
                    if first and k == 0:
                        mix_logits(0, 0)
                    if k == (4 if first else TENSOR_AT["turn_cw"]):
                        mix_turn_cw(c)
                    if not last:
                        if k == TENSOR_AT["turn_x"]:
                            mix_turn_x(c + 1)
                        if k == TENSOR_AT["bu"]:
                            mix_bu(c + 1)
                        if k == TENSOR_AT["c"]:
                            mix_c(c + 1)
                        if k == TENSOR_AT["turn_y"]:
                            mix_turn_y(c + 1, first)
                        if k == TENSOR_AT["turn_xe"]:
                            mix_turn_xe(c + 1)
                        if k == TENSOR_AT["logits"]:
                            mix_logits(c + 1, 1 - par)
                    if k == TENSOR_AT["turn_out"] and not first:
                        turn_out(c - 1, 1 - par, tail=last)

            for_chunks(pe, body)
            for k in range(UNITS - LAG, UNITS):
                down(NCHUNK - 1, k, False)
            turn_out(NCHUNK - 1, (NCHUNK - 1) % 2, last=True)

        @block.scalar
        def _(act):
            def round_piece(e, i):
                if i == 0:
                    act.wait_ge(w_loaded[e % 2], 48 * (e // 2 + 1))
                cols = slice(i * F, (i + 1) * F)
                nc.scalar.activation(w_hi[:, e, cols], stage[:, e % 2, cols], ACT.Copy).then_inc(w_hi_done, 1)

            def mix_hi_x(c):
                act.wait_ge(xn_turned, c + 1)
                nc.scalar.activation(act_hi[:], n_ps[:], ACT.Copy).then_inc(act_hi_ready, 1)

            def mix_du(c):
                nc.scalar.activation(y_sb[:], n_ps[:], ACT.Copy, scale=d_col[:]).then_inc(du_ready, 1)

            def mix_hi_w(c):
                act.wait_ge(w_ready, c + 1)
                nc.scalar.activation(act_hi[:], v_sb[:], ACT.Copy).then_inc(act_hi_ready, 1)

            def mix_z(c, tiles):
                if tiles[0] == 0:
                    act.wait_ge(shift_ready, c + 1)
                for j in tiles:
                    last = nc.scalar.activation(z_sb[:, j, :], n_ps[:, j * P:(j + 1) * P], ACT.Identity,
                                                bias=shift[:, j:j + 1], scale=rstd[:, j:j + 1])
                if tiles[-1] == NT - 1:
                    last.then_inc(z_ready, 1)

            def mix_hi_xe(c, par):
                act.wait_ge(xe_turned, c + 1)
                nc.scalar.activation(xe_hi[:, par, :], n_ps[:], ACT.Copy).then_inc(xe_hi_ready, 1)

            def mix_silus(c):
                act.wait_ge(lg_ready, c + 1)
                nc.scalar.activation(e_neg[:], lg[:], ACT.Silu, bias=-1.0)
                nc.scalar.activation(e_pos[:], lg[:], ACT.Silu, bias=1.0, scale=-1.0).then_inc(silus_ready, 1)

            def mix_cw_t(c, first):
                act.wait_ge(cw_turned, c + 1)
                if not first:
                    act.wait_ge(cw_stored, 16 * c)
                nc.scalar.activation(cw_t[:], n_ps[0:E * NT, 0:P], ACT.Copy).then_inc(cw_t_ready, 1)

            def fin_scale(c, tiles):
                if tiles[0] == 0:
                    act.wait_ge(fin_shift, c + 1)
                    act.wait_ge(out_free, 16 * (c + 1))
                for j in tiles:
                    last = nc.scalar.activation(o_sb[:, j, :], n_ps[:, j * P:(j + 1) * P], ACT.Identity,
                                                bias=shift2[:, j:j + 1], scale=rstd2[:, j:j + 1])
                if tiles[-1] == NT - 1:
                    last.then_inc(fin_z, 1)

            def silu(c, k, first):
                act.wait_ge(gu_ready, UNITS * c + k + 1)
                if not (first and k < 2):
                    act.wait_ge(hid_ready, UNITS * c + k - 1)
                nc.scalar.activation(gate[:, k % 2, :], g_ps[k % 2][:], ACT.Silu).then_inc(gate_ready, 1)

            def hid_high(c, k, first):
                act.wait_ge(hid_ready, UNITS * c + k + 1)
                if not (first and k < RING):
                    act.wait_ge(down_done, UNITS * c + k + 1 - RING)
                nc.scalar.activation(hid_hi[:, k % RING, :], hid[:, k % RING, :], ACT.Copy).then_inc(hi_ready, 1)

            act.wait_ge(const_ready, 4)
            nc.scalar.activation(ang[:, 6:7], ident[:, 0:1], ACT.Silu)
            act.wait_ge(small_loaded, 32)
            nc.scalar.activation(router[:, 0, :], proj[:, P + D:], ACT.Copy)
            nc.scalar.activation(proj_hi[:], proj[:, 0:P + D], ACT.Copy).then_inc(proj_split, 1)
            mix_hi_x(0)
            mix_du(0)
            for n in range(2 * PIECES):
                round_piece(n // PIECES, n % PIECES)
            mix_hi_w(0)
            for n in range(2 * PIECES, AHEAD * PIECES):
                round_piece(n // PIECES, n % PIECES)
            mix_z(0, (0, 1, 2, 3))
            mix_hi_xe(0, 0)

            def body(c, par, first, last):
                for k in range(UNITS):
                    silu(c, k, first)
                    if k >= 1:
                        hid_high(c, k - 1, first)
                    elif not first:
                        hid_high(c - 1, UNITS - 1, False)
                    if first and k % 2 == 1 and k // 2 < (E - AHEAD) * PIECES:
                        round_piece(AHEAD + k // 2 // PIECES, k // 2 % PIECES)
                    if first and k == 1:
                        mix_silus(0)
                    if k == (4 if first else SCALAR_AT["cw_t"]):
                        mix_cw_t(c, first)
                    if not last:
                        if k == SCALAR_AT["hi_x"]:
                            mix_hi_x(c + 1)
                        if k == SCALAR_AT["du"]:
                            mix_du(c + 1)
                        if k == SCALAR_AT["hi_w"]:
                            mix_hi_w(c + 1)
                        if k == SCALAR_AT["z_a"]:
                            mix_z(c + 1, (0, 1))
                        if k == SCALAR_AT["z_b"]:
                            mix_z(c + 1, (2, 3))
                        if k == SCALAR_AT["hi_xe"]:
                            mix_hi_xe(c + 1, 1 - par)
                        if k == SCALAR_AT["silus"]:
                            mix_silus(c + 1)
                    if not first:
                        if k == SCALAR_AT["fin_a"]:
                            fin_scale(c - 1, (0, 1))
                        if k == SCALAR_AT["fin_b"]:
                            fin_scale(c - 1, (2, 3))

            for_chunks(act, body)
            hid_high(NCHUNK - 1, UNITS - 1, False)
            fin_scale(NCHUNK - 1, (0, 1, 2, 3))

        @block.vector
        def _(dve):
            def measure(src, st, link):
                for j in range(NT):
                    last = nc.vector.bn_stats(st[:, j, :], src(j))
                last.then_inc(link, 1)

            def mean_var(st, m, ve, link, at):
                dve.wait_ge(link, at + 1)
                nc.vector.tensor_tensor(m[:], st[:, :, 1:3], st[:, :, 4:6], ALU.add)
                nc.vector.tensor_tensor(ve[:], st[:, :, 1], st[:, :, 4], ALU.subtract).then_inc(link, 1)
                dve.wait_ge(link, at + 2)
                nc.vector.tensor_tensor(m[:], m[:], pair_mean[:], ALU.mult)
                nc.vector.scalar_tensor_tensor(out=ve[:], in0=ve[:], scalar=0.25, in1=ve[:], op0=ALU.mult,
                                               op1=ALU.mult).then_inc(link, 1)
                dve.wait_ge(link, at + 3)
                return nc.vector.scalar_tensor_tensor(out=ve[:], in0=m[:, :, 1], scalar=LN_EPS, in1=ve[:],
                                                      op0=ALU.add, op1=ALU.add)

            def normalise(dst, src):
                for j in range(NT):
                    last = nc.vector.tensor_scalar(dst[:, j, :], src(j), mv[:, j, 0:1], rstd[:, j:j + 1],
                                                   ALU.subtract, ALU.mult)
                return last

            def shifts(dst, m, r):
                return nc.vector.scalar_tensor_tensor(out=dst[:], in0=m[:, :, 0], scalar=-1.0, in1=r[:],
                                                      op0=ALU.mult, op1=ALU.mult)

            def mix_stats_x(c):
                dve.wait_ge(x_loaded, 16 * (c + 1))
                measure(lambda j: x_sb[:, j, :], stats, mix_link)

            def mix_var(c, n):
                at = MIX_LINKS * c + (0, 5, 8)[n - 1]
                mean_var(stats, mv, var_eps, mix_link, at).then_inc(var_ready, 1)

            def mix_norm_x(c):
                dve.wait_ge(rstd_ready, 3 * c + 1)
                normalise(xn, lambda j: x_sb[:, j, :]).then_inc(xn_ready, 1)

            def mix_lo_x(c):
                dve.wait_ge(du_ready, c + 1)
                nc.vector.tensor_tensor(act_lo[:], n_ps[:], act_hi[:].bitcast(f32), ALU.subtract).then_inc(act_lo_ready, 1)

            def mix_enter(c):
                dve.wait_ge(bu_ready, c + 1)
                nc.vector.tensor_tensor(v_sb[:], m_ps[:], trig[:], ALU.mult).then_inc(mix_link, 1)

            def mix_scan(c):
                dve.wait_ge(mix_link, MIX_LINKS * c + 4)
                nc.vector.tensor_tensor_scan(sum_sb[:], v_sb[:], v_sb[:], 0.0, ALU.add, ALU.bypass).then_inc(mix_link, 1)

            def mix_leave(c):
                dve.wait_ge(mix_link, MIX_LINKS * c + 5)
                nc.vector.tensor_tensor(v_sb[:], sum_sb[:], trig[:], ALU.mult).then_inc(w_ready, 1)

            def mix_lo_w(c):
                dve.wait_ge(w_ready, c + 1)
                dve.wait_ge(act_hi_ready, 2 * c + 2)
                nc.vector.tensor_tensor(act_lo[:], v_sb[:], act_hi[:].bitcast(f32), ALU.subtract).then_inc(act_lo_ready, 1)

            def mix_y(c):
                dve.wait_ge(mixed_ready, c + 1)
                nc.vector.tensor_tensor(y_sb[:], m_ps[:], y_sb[:], ALU.add).then_inc(y_ready, 1)

            def mix_stats_y(c):
                dve.wait_ge(y_turned, c + 1)
                measure(lambda j: n_ps[:, j * P:(j + 1) * P], stats, mix_link)

            def mix_shift(c):
                dve.wait_ge(rstd_ready, 3 * c + 2)
                shifts(shift, mv, rstd).then_inc(shift_ready, 1)

            def mix_stats_x1(c, par):
                dve.wait_ge(x1_ready, c + 1)
                measure(lambda j: x1[:, par, j, :], stats, mix_link)

            def mix_norm_x1(c, par):
                dve.wait_ge(rstd_ready, 3 * c + 3)
                normalise(xn, lambda j: x1[:, par, j, :]).then_inc(xn_ready, 1)

            def mix_lo_xe(c, par):
                dve.wait_ge(xe_hi_ready, c + 1)
                nc.vector.tensor_tensor(xe_lo[:, par, :], n_ps[:], xe_hi[:, par, :].bitcast(f32), ALU.subtract).then_inc(xe_lo_ready, 1)

            def groups(t):
                return t[:].rearrange("p j r e -> p (j r) e")

            def wide(t, n):
                return t.unsqueeze(2).broadcast_to([P, t.shape[1], n])

            def mix_softmax_in(c):
                at = SOFT_LINKS * c
                pair = "p j r -> p (j r)"
                dve.wait_ge(logits_ready, c + 1)
                nc.vector.tensor_reduce(out=lg[:].rearrange("p j r e -> p j (r e)"),
                                        in_=m_ps[:, 0:NT * 4 * E].rearrange("p (j h q) -> p j q h", j=NT, h=2),
                                        op=ALU.add, axis=AX.X).then_inc(raw_read, 1)
                dve.wait_ge(raw_read, c + 1)
                nc.vector.tensor_reduce(out=gmax[:].rearrange(pair), in_=groups(lg), op=ALU.max,
                                        axis=AX.X).then_inc(soft_link, 1)
                dve.wait_ge(soft_link, at + 1)
                nc.vector.tensor_tensor(groups(lg), groups(lg), wide(gmax[:].rearrange(pair), E),
                                        ALU.subtract).then_inc(soft_link, 1)
                dve.wait_ge(soft_link, at + 2)
                nc.vector.tensor_tensor(lg[:], lg[:], sharp[:], ALU.mult).then_inc(lg_ready, 1)

            def mix_exps(c):
                at = SOFT_LINKS * c + 2
                dve.wait_ge(silus_ready, c + 1)
                nc.vector.reciprocal(e_pos[:], e_pos[:]).then_inc(soft_link, 1)
                dve.wait_ge(soft_link, at + 1)
                nc.vector.scalar_tensor_tensor(out=groups(lg), in0=groups(e_neg), scalar=-1.0, in1=groups(e_pos),
                                               op0=ALU.mult, op1=ALU.mult).then_inc(soft_link, 1)

            def mix_products(c):
                at = SOFT_LINKS * c + 4
                dve.wait_ge(soft_link, at)
                nc.vector.tensor_tensor(pr[:], lg[:, :, 0, :], lg[:, :, 1, :], ALU.mult)
                nc.vector.tensor_reduce(out=gsum[:].rearrange("p j r -> p (j r)"), in_=groups(lg), op=ALU.add,
                                        axis=AX.X).then_inc(soft_link, 1)
                dve.wait_ge(soft_link, at + 1)
                nc.vector.tensor_reduce(out=psum_[:], in_=pr[:], op=ALU.add, axis=AX.X)
                nc.vector.tensor_tensor(den[:], gsum[:, :, 0], gsum[:, :, 1], ALU.mult).then_inc(soft_link, 1)

            def mix_weights(c):
                at = SOFT_LINKS * c + 6
                dve.wait_ge(soft_link, at)
                nc.vector.scalar_tensor_tensor(out=den[:], in0=den[:], scalar=MIX_EPS, in1=psum_[:],
                                               op0=ALU.mult, op1=ALU.add).then_inc(soft_link, 1)
                dve.wait_ge(soft_link, at + 1)
                nc.vector.reciprocal(den[:], den[:]).then_inc(soft_link, 1)
                dve.wait_ge(soft_link, at + 2)
                nc.vector.tensor_tensor(cw_pad[:, 0:E * NT].rearrange("p (e j) -> p j e", j=NT), pr[:],
                                        wide(den[:], E), ALU.mult).then_inc(cw_ready, 1)

            def fin_stats(c):
                dve.wait_ge(fin_turned, c + 1)
                measure(lambda j: n_ps[:, j * P:(j + 1) * P], stats2, fin_link)

            def fin_mean_var(c):
                mean_var(stats2, mv2, var_eps2, fin_link, FIN_LINKS * c).then_inc(fin_var, 1)

            def fin_shifts(c):
                dve.wait_ge(fin_rstd, c + 1)
                shifts(shift2, mv2, rstd2).then_inc(fin_shift, 1)

            def hidden(c, k, first):
                dve.wait_ge(gate_ready, UNITS * c + k + 1)
                if not (first and k < RING):
                    cc, kk = (c, k - RING) if k >= RING else (c - 1, k - RING + UNITS)
                    if on_pool(kk):
                        dve.wait_ge(lo_pool, N_POOL_LO * cc + lo_count(kk))
                    else:
                        dve.wait_ge(lo_dve, N_DVE_LO * cc + lo_count(kk))
                nc.vector.tensor_tensor(hid[:, k % RING, :], gate[:, k % 2, :], u_ps[k % 2][:], ALU.mult).then_inc(hid_ready, 1)

            def hid_low(c, k, first):
                if on_pool(k):
                    return
                dve.wait_ge(hi_ready, UNITS * c + k + 1)
                nc.vector.tensor_tensor(hid_lo[:, k % RING, :], hid[:, k % RING, :], hid_hi[:, k % RING, :].bitcast(f32),
                                        ALU.subtract).then_inc(lo_dve, 1)

            def weigh(c, par, e, first):
                dve.wait_ge(down_done, UNITS * c + NB * (e + 1))
                dve.wait_ge(cw_spread[e % 4], 16 * (2 * c + e // 4 + 1))
                if e > 0 and not (first and e < 3):
                    dve.wait_ge(part_added, ADDS * c + max(e - 2, 0))
                dst = acc[:, par, :] if e == 0 else y_part[:, e % 2, :]
                nc.vector.tensor_tensor(dst, y_ps[e % 2][:], cw_b[:, e % 4, :], ALU.mult).then_inc(part_ready, 1)

            links = [0]

            def then(ins):
                links[0] += 1
                ins.then_inc(trig_link, 1)
                dve.wait_ge(trig_link, links[0])

            w, w2, r, co, si, t0 = (ang[:, i:i + 1] for i in range(6))
            nc.vector.memset(half[:], -0.5).then_inc(out_free, 16)
            nc.vector.memset(pair_mean[:, :, 0], 0.5)
            nc.vector.memset(pair_mean[:, :, 1], 1.0 / D)
            nc.vector.memset(sharp[:, :, 0, :], 1.0)
            nc.vector.memset(sharp[:, :, 1, :], GATE_SHARP)
            nc.vector.memset(cw_pad[:], 0.0).then_inc(const_ready, 1)
            slope = sum_sb
            spare = z_sb[:].rearrange("p j d -> p (j d)")
            nc.vector.memset(trig[0:NS, 0:1], 1.0)
            nc.vector.memset(trig[NS:P, 0:1], 0.0)
            nc.vector.memset(slope[0:NS, 0:1], 0.0)
            nc.vector.memset(slope[NS:P, 0:1], 1.0)
            dve.wait_ge(const_ready, 2)
            dve.wait_ge(omega_ready, 1)
            then(nc.vector.tensor_copy(w, m_ps[:, 0:1]))
            then(nc.vector.tensor_tensor(w2, w, w, ALU.mult))
            nc.vector.tensor_scalar(co, w2, -1.0, 1.0, ALU.mult, ALU.add)
            then(nc.vector.tensor_scalar(r, w2, 1.0, None, ALU.add))
            then(nc.vector.reciprocal(r, r))
            nc.vector.scalar_tensor_tensor(out=si, in0=w, scalar=-2.0, in1=r, op0=ALU.mult, op1=ALU.mult)
            then(nc.vector.tensor_tensor(co, co, r, ALU.mult))
            mix_stats_x(0)
            mix_var(0, 1)
            n = 1
            while n < SEQ:
                if n in (1, 4):
                    then(nc.vector.tensor_tensor(w, si, si, ALU.mult))
                    then(nc.vector.scalar_tensor_tensor(out=w, in0=co, scalar=co, in1=w, op0=ALU.mult, op1=ALU.add))
                    then(nc.vector.tensor_scalar(w, w, -0.5, 1.5, ALU.mult, ALU.add))
                    nc.vector.tensor_tensor(co, co, w, ALU.mult)
                    then(nc.vector.tensor_tensor(si, si, w, ALU.mult))
                old, new = slice(0, n), slice(n, 2 * n)
                if n == SEQ // 2:
                    then(nc.vector.tensor_scalar(v_sb[:, old], slope[:, old], si, None, ALU.mult))
                    nc.vector.scalar_tensor_tensor(out=trig[:, new], in0=trig[:, old], scalar=co, in1=v_sb[:, old],
                                                   op0=ALU.mult, op1=ALU.add).then_inc(trig_ready, 1)
                    break
                nc.vector.tensor_scalar(v_sb[:, old], slope[:, old], si, None, ALU.mult)
                nc.vector.tensor_scalar(spare[:, old], trig[:, old], si, None, ALU.mult)
                then(nc.vector.tensor_tensor(w, si, si, ALU.mult))
                nc.vector.scalar_tensor_tensor(out=trig[:, new], in0=trig[:, old], scalar=co, in1=v_sb[:, old],
                                               op0=ALU.mult, op1=ALU.add)
                nc.vector.scalar_tensor_tensor(out=slope[:, new], in0=slope[:, old], scalar=co, in1=spare[:, old],
                                               op0=ALU.mult, op1=ALU.subtract)
                then(nc.vector.scalar_tensor_tensor(out=si, in0=si, scalar=2.0, in1=co, op0=ALU.mult, op1=ALU.mult))
                then(nc.vector.scalar_tensor_tensor(out=co, in0=co, scalar=co, in1=w, op0=ALU.mult, op1=ALU.subtract))
                if n == 4:
                    mix_norm_x(0)
                if n == 32:
                    dve.wait_ge(small_loaded, 32)
                    dve.wait_ge(proj_split, 1)
                    nc.vector.tensor_tensor(router[:, 1, :], proj[:, P + D:], router[:, 0, :].bitcast(f32), ALU.subtract)
                    nc.vector.tensor_tensor(proj_lo[:], proj[:, 0:P + D], proj_hi[:].bitcast(f32),
                                            ALU.subtract).then_inc(proj_split, 1)
                    mix_lo_x(0)
                n *= 2
            dve.wait_ge(trig_ready, 1)
            mix_enter(0)
            mix_scan(0)
            mix_leave(0)
            mix_lo_w(0)
            mix_y(0)
            mix_stats_y(0)
            mix_var(0, 2)
            mix_shift(0)
            dve.wait_ge(z_ready, 1)
            nc.vector.tensor_tensor(x1[:, 0], x_sb[:], z_sb[:], ALU.add).then_inc(x1_ready, 1)
            mix_stats_x1(0, 0)
            mix_var(0, 3)
            mix_norm_x1(0, 0)
            mix_lo_xe(0, 0)

            def body(c, par, first, last):
                for k in range(UNITS):
                    hidden(c, k, first)
                    if k >= 1:
                        hid_low(c, k - 1, first)
                    elif not first:
                        hid_low(c - 1, UNITS - 1, False)
                    if first and k == 0:
                        mix_softmax_in(0)
                    if first and k == 1:
                        mix_exps(0)
                        mix_products(0)
                    if k == (2 if first else VECTOR_AT["weights"]):
                        mix_weights(c)
                    if k % NB == 0 and k >= 8:
                        weigh(c, par, k // NB - 2, first)
                    if k in (0, 4) and not first:
                        weigh(c - 1, 1 - par, E - 2 + k // NB, False)
                    if not last:
                        if k == VECTOR_AT["stats_x"]:
                            mix_stats_x(c + 1)
                        if k == VECTOR_AT["var_x"]:
                            mix_var(c + 1, 1)
                        if k == VECTOR_AT["norm_x"]:
                            mix_norm_x(c + 1)
                        if k == VECTOR_AT["lo_x"]:
                            mix_lo_x(c + 1)
                        if k == VECTOR_AT["enter"]:
                            mix_enter(c + 1)
                        if k == VECTOR_AT["scan"]:
                            mix_scan(c + 1)
                        if k == VECTOR_AT["leave"]:
                            mix_leave(c + 1)
                        if k == VECTOR_AT["lo_w"]:
                            mix_lo_w(c + 1)
                        if k == VECTOR_AT["y"]:
                            mix_y(c + 1)
                        if k == VECTOR_AT["stats_y"]:
                            mix_stats_y(c + 1)
                        if k == VECTOR_AT["var_y"]:
                            mix_var(c + 1, 2)
                        if k == VECTOR_AT["shift"]:
                            mix_shift(c + 1)
                        if k == VECTOR_AT["stats_x1"]:
                            mix_stats_x1(c + 1, 1 - par)
                        if k == VECTOR_AT["var_x1"]:
                            mix_var(c + 1, 3)
                        if k == VECTOR_AT["norm_x1"]:
                            mix_norm_x1(c + 1, 1 - par)
                        if k == VECTOR_AT["lo_xe"]:
                            mix_lo_xe(c + 1, 1 - par)
                        if k == VECTOR_AT["softmax"]:
                            mix_softmax_in(c + 1)
                        if k == VECTOR_AT["exps"]:
                            mix_exps(c + 1)
                        if k == VECTOR_AT["products"]:
                            mix_products(c + 1)
                    if not first:
                        if k == VECTOR_AT["fin_stats"]:
                            fin_stats(c - 1)
                        if k == VECTOR_AT["fin_var"]:
                            fin_mean_var(c - 1)
                        if k == VECTOR_AT["fin_shift"]:
                            fin_shifts(c - 1)

            for_chunks(dve, body)
            weigh(NCHUNK - 1, (NCHUNK - 1) % 2, E - 2, False)
            hid_low(NCHUNK - 1, UNITS - 1, False)
            weigh(NCHUNK - 1, (NCHUNK - 1) % 2, E - 1, False)
            fin_stats(NCHUNK - 1)
            fin_mean_var(NCHUNK - 1)
            fin_shifts(NCHUNK - 1)

        @block.gpsimd
        def _(pool):
            def split_piece(e, i):
                pool.wait_ge(w_hi_done, PIECES * e + i + 1)
                cols = slice(i * F, (i + 1) * F)
                nc.gpsimd.tensor_tensor(w_lo[:, e, cols], stage[:, e % 2, cols], w_hi[:, e, cols].bitcast(f32),
                                        ALU.subtract).then_inc(w_lo_done, 1)

            def mix_rstd(c, n):
                pool.wait_ge(var_ready, 3 * c + n)
                nc.gpsimd.tensor_tensor(rstd[:], var_eps[:], half[:], ALU.pow).then_inc(rstd_ready, 1)

            def mix_residual(c, par):
                pool.wait_ge(z_ready, c + 1)
                nc.gpsimd.tensor_tensor(x1[:, par], x_sb[:], z_sb[:], ALU.add).then_inc(x1_ready, 1)

            def fin_rsqrt(c):
                pool.wait_ge(fin_var, c + 1)
                nc.gpsimd.tensor_tensor(rstd2[:], var_eps2[:], half[:], ALU.pow).then_inc(fin_rstd, 1)

            def fin_residual(c, par):
                pool.wait_ge(fin_z, c + 1)
                nc.gpsimd.tensor_tensor(o_sb[:], x1[:, par], o_sb[:], ALU.add).then_inc(fin_ready, 1)

            def hid_low(c, k, first):
                if not on_pool(k):
                    return
                pool.wait_ge(hi_ready, UNITS * c + k + 1)
                nc.gpsimd.tensor_tensor(hid_lo[:, k % RING, :], hid[:, k % RING, :], hid_hi[:, k % RING, :].bitcast(f32),
                                        ALU.subtract).then_inc(lo_pool, 1)

            def add_part(c, par, e):
                pool.wait_ge(part_ready, E * c + e + 1)
                if e > 1:
                    pool.wait_ge(part_added, ADDS * c + e - 1)
                nc.gpsimd.tensor_tensor(acc[:, par, :], acc[:, par, :], y_part[:, e % 2, :], ALU.add).then_inc(part_added, 1)

            nc.gpsimd.memset(ident[:], 0.0).then_inc(const_ready, 1)
            pool.wait_ge(const_ready, 2)
            nc.gpsimd.affine_select(out=ident[:], in_=ident[:], compare_op=ALU.not_equal, fill=1.0, base=0,
                                    pattern=[[-1, P]], channel_multiplier=1).then_inc(const_ready, 2)
            mix_rstd(0, 1)
            for n in range(3 * PIECES):
                split_piece(n // PIECES, n % PIECES)
            mix_rstd(0, 2)
            mix_rstd(0, 3)
            for n in range(3 * PIECES, AHEAD * PIECES):
                split_piece(n // PIECES, n % PIECES)

            def body(c, par, first, last):
                for k in range(UNITS):
                    if k >= 1:
                        hid_low(c, k - 1, first)
                    elif not first:
                        hid_low(c - 1, UNITS - 1, False)
                    if k % NB == 0 and k >= 12:
                        add_part(c, par, k // NB - 2)
                    if k in (0, 4) and not first:
                        add_part(c - 1, 1 - par, E - 2 + k // NB)
                    if first and k % 2 == 1 and k // 2 < (E - AHEAD) * PIECES:
                        split_piece(AHEAD + k // 2 // PIECES, k // 2 % PIECES)
                    if not last:
                        if k == GPSIMD_AT["rstd_x"]:
                            mix_rstd(c + 1, 1)
                        if k == GPSIMD_AT["rstd_y"]:
                            mix_rstd(c + 1, 2)
                        if k == GPSIMD_AT["residual"]:
                            mix_residual(c + 1, 1 - par)
                        if k == GPSIMD_AT["rstd_x1"]:
                            mix_rstd(c + 1, 3)
                    if not first:
                        if k == GPSIMD_AT["fin_rstd"]:
                            fin_rsqrt(c - 1)
                        if k == GPSIMD_AT["fin_add"]:
                            fin_residual(c - 1, 1 - par)

            for_chunks(pool, body)
            hid_low(NCHUNK - 1, UNITS - 1, False)
            add_part(NCHUNK - 1, (NCHUNK - 1) % 2, E - 2)
            add_part(NCHUNK - 1, (NCHUNK - 1) % 2, E - 1)
            fin_rsqrt(NCHUNK - 1)
            fin_residual(NCHUNK - 1, (NCHUNK - 1) % 2)


def sine_rows():
    m = np.arange(NS)
    source = np.where(m <= NS // 2, m - 1, NS - m)
    sign = np.where(m <= NS // 2, 1.0, -1.0) * (m > 0)
    wave = -np.sin(2.0 * np.pi * ((m[:, None] * m[None, :]) % NS) / NS)
    rows = np.zeros((NS // 2, NS))
    for i in range(1, NS):
        rows[source[i]] += sign[i] * wave[i]
    return np.concatenate([rows, rows], axis=1).astype(np.float32)


def kernel(L0_attn_u, L0_attn_a_params, L0_attn_B_w, L0_attn_C_w, L0_attn_D, L0_ffn_w_router, L0_ffn_w_gating,
           L0_ffn_w_gate, L0_ffn_w_up, L0_ffn_w_down):
    import concourse.bacc as bacc
    from concourse.bass_utils import run_bass_kernel_spmd

    b_t, c_t = np.asarray(L0_attn_B_w).T, np.asarray(L0_attn_C_w).T
    arrays = {
        "x_in": L0_attn_u,
        "proj_in": np.concatenate([b_t, b_t, np.concatenate([c_t, c_t], axis=0), L0_ffn_w_router, L0_ffn_w_gating], axis=1),
        "a_in": np.asarray(L0_attn_a_params).reshape(NS // 2, 1),
        "sines_in": sine_rows(),
        "d_in": np.asarray(L0_attn_D).reshape(D, 1),
        "wgate_in": L0_ffn_w_gate,
        "wup_in": L0_ffn_w_up,
        "wdown_in": L0_ffn_w_down,
    }
    arrays = {n: np.ascontiguousarray(a) for n, a in arrays.items()}
    nc = bacc.Bacc("TRN2", target_bir_lowering=False, num_devices=1)
    args = [nc.dram_tensor(n, a.shape, mybir.dt.from_np(a.dtype), kind="ExternalInput").ap() for n, a in arrays.items()]
    args.append(nc.dram_tensor("x_out", (NCHUNK, SEQ, D), mybir.dt.float32, kind="ExternalOutput").ap())
    build(nc, *args)
    return run_bass_kernel_spmd(nc, [arrays], core_ids=[0]).results[0]["x_out"]
```

```python
from contextlib import ExitStack

import numpy as np

import concourse.bass as bass
from concourse import mybir

P = 128
NCHUNK, SEQ, D = 16, 512, 128
NT = SEQ // P
NS = 64
E, F = 8, 512
NB = F // P
UNITS = E * NB
WCOLS = 3 * F
LAG = 3
RING = 4
GATE_SHARP = 10.0
AHEAD = 4
PIECES = WCOLS // F
TENSOR_AT = {"turn_cw": 4, "turn_x": 5, "bu": 9, "turn_out": 10, "c": 15, "turn_y": 16, "turn_xe": 26,
             "logits": 27}
SCALAR_AT = {"cw_t": 3, "hi_x": 8, "du": 8, "hi_w": 13, "fin_a": 14, "fin_b": 15, "z_a": 18, "z_b": 18,
             "hi_xe": 26, "silus": 28}
VECTOR_AT = {"weights": 1, "stats_x": 1, "var_x": 2, "norm_x": 3, "lo_x": 7, "enter": 8, "scan": 9,
             "fin_stats": 10, "fin_var": 10, "fin_shift": 11, "leave": 12, "lo_w": 13, "y": 15, "stats_y": 16, "var_y": 16,
             "shift": 18, "stats_x1": 22, "var_x1": 22, "norm_x1": 24, "lo_xe": 26, "softmax": 27, "exps": 30,
             "products": 31}
GPSIMD_AT = {"rstd_x": 2, "fin_rstd": 11, "fin_add": 14, "rstd_y": 16, "residual": 18, "rstd_x1": 22}
LN_EPS = 1e-5
MIX_EPS = 1e-9
HALF = SEQ // 2
WARM = (13, 3, 6, 18, 3)
SPLIT_BEFORE = (8, 10)
SMALL = 32
PROJ = P + D + 2 * E

POOL_LO = (1, 3)


def on_pool(k):
    return k % 4 in POOL_LO


N_POOL_LO = sum(on_pool(k) for k in range(UNITS))
N_DVE_LO = UNITS - N_POOL_LO


def lo_count(k):
    return sum(on_pool(j) == on_pool(k) for j in range(k + 1))


def build(nc, x_in, proj_in, a_in, sines_in, d_in, wgate_in, wup_in, wdown_in, out):
    f32, f32r = mybir.dt.float32, mybir.dt.float32r
    ALU, ACT, AX = mybir.AluOpType, mybir.ActivationFunctionType, mybir.AxisListType

    x_tok = x_in.rearrange("b (j p) d -> b p j d", p=P)
    out_tok = out.rearrange("b (j p) d -> b p j d", p=P)
    wdown_v = wdown_in.rearrange("e (b p) h -> e p b h", p=P)
    cw_dram = nc.dram_tensor("cw_scratch", [2, E * NT, P], f32, kind="Internal").ap()

    with ExitStack() as ctx:
        def sb(name, shape, dt=f32):
            return ctx.enter_context(nc.sbuf_tensor(name, shape, dt))

        def ps(name):
            return ctx.enter_context(nc.psum_tensor(name, [P, SEQ], f32))

        def sem(name):
            return ctx.enter_context(nc.semaphore(name))

        ident = sb("ident", [P, P])
        half = sb("half", [P, NT])
        pair_mean = sb("pair_mean", [P, NT, 2])
        sharp = sb("sharp", [P, NT, 2, E])
        proj = sb("proj", [P, PROJ])
        proj_hi, proj_lo = sb("proj_hi", [P, P + D], f32r), sb("proj_lo", [P, P + D], f32r)
        router = sb("router", [P, 2, 2 * E], f32r)
        a_col, sines = sb("a_col", [NS // 2, 1]), sb("sines", [NS // 2, P])
        d_col = sb("d_col", [P, 1])
        ang = sb("ang", [P, 8])
        low = sb("low", [P, 2, SMALL + 1])
        high = sb("high", [P, 2, 4])
        trig = sb("trig", [P, SEQ])
        stage = sb("stage", [P, 2, WCOLS])
        w_hi, w_lo = sb("w_hi", [P, E, WCOLS], f32r), sb("w_lo", [P, E, WCOLS], f32r)
        x_sb = sb("x_sb", [P, NT, D])
        stats, mv = sb("stats", [P, NT, 6]), sb("mv", [P, NT, 2])
        var_eps, rstd, shift = sb("var_eps", [P, NT]), sb("rstd", [P, NT]), sb("shift", [P, NT])
        xn = sb("xn", [P, NT, D])
        act_hi, act_lo = sb("act_hi", [P, SEQ], f32r), sb("act_lo", [P, SEQ], f32r)
        y_sb = sb("y_sb", [P, SEQ])
        v_sb, sum_sb = sb("v_sb", [P, SEQ]), sb("sum_sb", [P, SEQ])
        z_sb = sb("z_sb", [P, NT, D])
        x1 = sb("x1", [P, 2, NT, D])
        lg, e_neg, e_pos = (sb(n, [P, NT, 2, E]) for n in ("lg", "e_neg", "e_pos"))
        gmax, gsum = sb("gmax", [P, NT, 2]), sb("gsum", [P, NT, 2])
        pr, psum_, den = sb("pr", [P, NT, E]), sb("psum_", [P, NT]), sb("den", [P, NT])
        cw_pad = sb("cw_pad", [P, P])
        cw_t = sb("cw_t", [E * NT, P])
        xe_hi, xe_lo = sb("xe_hi", [P, 2, SEQ], f32r), sb("xe_lo", [P, 2, SEQ], f32r)
        gate = sb("gate", [P, 2, SEQ])
        hid = sb("hid", [P, RING, SEQ])
        hid_hi, hid_lo = sb("hid_hi", [P, RING, SEQ], f32r), sb("hid_lo", [P, RING, SEQ], f32r)
        cw_b = sb("cw_b", [P, 4, SEQ])
        y_part = sb("y_part", [P, 2, SEQ])
        acc = sb("acc", [P, 2, SEQ])
        stats2, mv2 = sb("stats2", [P, NT, 6]), sb("mv2", [P, NT, 2])
        var_eps2, rstd2, shift2 = sb("var_eps2", [P, NT]), sb("rstd2", [P, NT]), sb("shift2", [P, NT])
        o_sb = sb("o_sb", [P, NT, D])

        g_ps, u_ps = [ps("g0"), ps("g1")], [ps("u0"), ps("u1")]
        y_ps = [ps("y0"), ps("y1")]
        m_ps = ps("m_ps")
        n_ps = ps("n_ps")

        angle_loaded, x_loaded, small_loaded, out_free = sem("angle_loaded"), sem("x_loaded"), sem("small_loaded"), sem("out_free")
        w_loaded = [sem("w_loaded0"), sem("w_loaded1")]
        w_hi_done, w_lo_done = sem("w_hi_done"), sem("w_lo_done")
        const_ready = sem("const_ready")
        proj_split, omega_ready, trig_link, trig_ready = sem("proj_split"), sem("omega_ready"), sem("trig_link"), sem("trig_ready")
        cw_stored, cw_spread = sem("cw_stored"), [sem(f"cw_spread{i}") for i in range(4)]
        mix_link = sem("mix_link")
        soft_link = sem("soft_link")
        var_ready, rstd_ready = sem("var_ready"), sem("rstd_ready")
        xn_ready, xn_turned = sem("xn_ready"), sem("xn_turned")
        act_hi_ready, act_lo_ready, du_ready = sem("act_hi_ready"), sem("act_lo_ready"), sem("du_ready")
        bu_ready, w_ready, mixed_ready, y_ready = sem("bu_ready"), sem("w_ready"), sem("mixed_ready"), sem("y_ready")
        y_turned, shift_ready, z_ready, x1_ready = sem("y_turned"), sem("shift_ready"), sem("z_ready"), sem("x1_ready")
        xe_turned, xe_hi_ready, xe_lo_ready = sem("xe_turned"), sem("xe_hi_ready"), sem("xe_lo_ready")
        logits_ready, raw_read, lg_ready, silus_ready = sem("logits_ready"), sem("raw_read"), sem("lg_ready"), sem("silus_ready")
        cw_ready, cw_turned, cw_t_ready = sem("cw_ready"), sem("cw_turned"), sem("cw_t_ready")
        xn_tile, z_tile, x1_tile, fin_tile = sem("xn_tile"), sem("z_tile"), sem("x1_tile"), sem("fin_tile")
        w_half, act_hi_half, warmed = sem("w_half"), sem("act_hi_half"), sem("warmed")
        g_done, u_done, gate_ready, hid_ready = sem("g_done"), sem("u_done"), sem("gate_ready"), sem("hid_ready")
        hi_ready, lo_dve, lo_pool = sem("hi_ready"), sem("lo_dve"), sem("lo_pool")
        down_done, part_ready, part_added = sem("down_done"), sem("part_ready"), sem("part_added")
        fin_link, fin_turned, fin_var, fin_rstd = sem("fin_link"), sem("fin_turned"), sem("fin_var"), sem("fin_rstd")
        fin_shift, fin_z, fin_ready = sem("fin_shift"), sem("fin_z"), sem("fin_ready")

        MIX_LINKS, SOFT_LINKS, FIN_LINKS, ADDS = 11, 8, 3, E - 1

        def for_chunks(eng, body):
            body(0, 0, True, False)
            with eng.Fori(0, (NCHUNK - 2) // 2) as i:
                body(2 * i + 1, 1, False, False)
                body(2 * i + 2, 0, False, False)
            body(NCHUNK - 1, (NCHUNK - 1) % 2, False, True)

        block = ctx.enter_context(nc.Block())

        @block.sync
        def _(sp):
            def load_x(c):
                sp.dma_start(x_sb[:], x_tok[c]).then_inc(x_loaded, 16)

            def load_expert(e):
                if e >= 2:
                    sp.wait_ge(w_lo_done, PIECES * (e - 1))
                s = e % 2
                sp.dma_start(stage[:, s, 0:F], wgate_in[e]).then_inc(w_loaded[s], 16)
                sp.dma_start(stage[:, s, F:2 * F], wup_in[e]).then_inc(w_loaded[s], 16)
                sp.dma_start(stage[:, s, 2 * F:].rearrange("p (b h) -> p b h", b=NB),
                             wdown_v[e]).then_inc(w_loaded[s], 16)

            def store_cw(c, par):
                sp.wait_ge(cw_t_ready, c + 1)
                sp.dma_start(cw_dram[par], cw_t[:]).then_inc(cw_stored, 16)

            def spread_cw(c, par, e, first):
                if e == 0:
                    sp.wait_ge(cw_stored, 16 * (c + 1))
                if not (first and e < 4):
                    sp.wait_ge(part_ready, E * c + e - 3)
                row = cw_dram[par, e * NT:(e + 1) * NT, :].rearrange("j p -> (j p)")
                row = row.rearrange("(a t) -> a t", a=1).broadcast_to([P, SEQ])
                sp.dma_start(cw_b[:, e % 4, :], row).then_inc(cw_spread[e % 4], 16)

            def store_out(c):
                sp.wait_ge(fin_ready, c + 1)
                sp.dma_start(out_tok[c], o_sb[:]).then_inc(out_free, 16)

            sp.dma_start(a_col[:], a_in).then_inc(angle_loaded, 16)
            sp.dma_start(sines[:], sines_in).then_inc(angle_loaded, 16)
            load_x(0)
            sp.dma_start(proj[:], proj_in).then_inc(small_loaded, 16)
            sp.dma_start(d_col[:], d_in).then_inc(small_loaded, 16)
            for e in range(AHEAD + 2):
                load_expert(e)

            def body(c, par, first, last):
                if not last:
                    sp.wait_ge(x1_ready, c + 1)
                    load_x(c + 1)
                store_cw(c, par)
                for e in range(E):
                    spread_cw(c, par, e, first)
                    if e == 4 and not first:
                        store_out(c - 1)
                    if first and e + AHEAD + 2 < E:
                        load_expert(e + AHEAD + 2)

            for_chunks(sp, body)
            store_out(NCHUNK - 1)
            sp.wait_ge(out_free, 16 * (NCHUNK + 1))
            sp.wait_ge(cw_stored, 16 * NCHUNK)

        @block.tensor
        def _(pe):
            def exact(dst, w_h, w_l, x_h, x_l, start=True, stop=True):
                nc.tensor.matmul(dst, w_h, x_h, start=start, stop=False)
                nc.tensor.matmul(dst, w_h, x_l, start=False, stop=False)
                return nc.tensor.matmul(dst, w_l, x_h, start=False, stop=stop)

            def turn(dst, src):
                for j in range(NT):
                    last = nc.tensor.transpose(dst[:, j * P:(j + 1) * P], src(j), ident[:])
                return last

            def turn_tiles(n):
                for j in range(NT):
                    if j < NT - 1:
                        pe.wait_ge(xn_tile, (NT - 1) * n + j + 1)
                    else:
                        pe.wait_ge(xn_ready, n + 1)
                    last = nc.tensor.transpose(n_ps[:, j * P:(j + 1) * P], xn[:, j, :], ident[:])
                return last

            def keep_warm(n):
                for i in range(n):
                    last = nc.tensor.matmul(y_ps[1][:, 0:2 * P].rearrange("p (a b) -> p a b", a=2), ident[:],
                                            ident[:].unsqueeze(1).broadcast_to([P, 2, P]), start=True, stop=True)
                return last

            def mix_turn_x(c):
                pe.wait_ge(xn_ready, 2 * c + 1)
                pe.wait_ge(cw_t_ready, c)
                turn(n_ps, lambda j: xn[:, j, :]).then_inc(xn_turned, 1)

            def mix_bu(c, prologue=False):
                if prologue:
                    pe.wait_ge(trig_link, 1)
                else:
                    pe.wait_ge(raw_read, c)
                pe.wait_ge(act_hi_ready, 2 * c + 1)
                pe.wait_ge(act_lo_ready, 2 * c + 1)
                exact(m_ps[:], proj_hi[:, 0:P], proj_lo[:, 0:P], act_hi[:], act_lo[:]).then_inc(bu_ready, 1)

            def mix_c(c):
                pe.wait_ge(act_hi_ready, 2 * c + 2)
                pe.wait_ge(act_lo_ready, 2 * c + 2)
                exact(m_ps[:], proj_hi[:, P:P + D], proj_lo[:, P:P + D], act_hi[:], act_lo[:]).then_inc(mixed_ready, 1)

            def mix_turn_y(c, first):
                pe.wait_ge(y_ready, c + 1)
                if not first:
                    pe.wait_ge(fin_z, c - 1)
                turn(n_ps, lambda j: y_sb[:, j * P:(j + 1) * P]).then_inc(y_turned, 1)

            def mix_turn_xe(c):
                pe.wait_ge(xn_ready, 2 * c + 2)
                turn(n_ps, lambda j: xn[:, j, :]).then_inc(xe_turned, 1)

            def mix_logits(c, par):
                pe.wait_ge(xe_hi_ready, c + 1)
                pe.wait_ge(xe_lo_ready, c + 1)
                for j in range(NT):
                    t, at = slice(j * P, (j + 1) * P), 4 * E * j
                    nc.tensor.matmul(m_ps[:, at:at + 4 * E], xe_hi[:, par, t], router[:], start=True, stop=False)
                    last = nc.tensor.matmul(m_ps[:, at:at + 2 * E], xe_lo[:, par, t], router[:, 0, :], start=False, stop=True)
                last.then_inc(logits_ready, 1)

            def mix_turn_cw(c):
                pe.wait_ge(cw_ready, c + 1)
                nc.tensor.transpose(n_ps[:, 0:P], cw_pad[:], ident[:]).then_inc(cw_turned, 1)

            def turn_out(c, par, tail=False, last=False):
                pe.wait_ge(part_added, ADDS * (c + 1))
                if last:
                    pe.wait_ge(fin_z, c)
                elif tail:
                    pe.wait_ge(cw_t_ready, c + 2)
                else:
                    pe.wait_ge(act_lo_ready, 2 * c + 5)
                turn(n_ps, lambda j: acc[:, par, j * P:(j + 1) * P]).then_inc(fin_turned, 1)

            def gate_up(c, par, k, first):
                e, b, buf = k // NB, k % NB, k % 2
                if first and b == 0:
                    pe.wait_ge(w_lo_done, PIECES * (e + 1))
                for dst, off, used, done in ((g_ps[buf], 0, gate_ready, g_done), (u_ps[buf], F, hid_ready, u_done)):
                    if not (first and k < 2):
                        pe.wait_ge(used, UNITS * c + k - 1)
                    cols = slice(off + b * P, off + (b + 1) * P)
                    exact(dst[:], w_hi[:, e, cols], w_lo[:, e, cols], xe_hi[:, par, :],
                          xe_lo[:, par, :]).then_inc(done, 1)

            def down(c, k, first, last_unit=False):
                e, b = k // NB, k % NB
                pe.wait_ge(hi_ready, UNITS * c + k + 1)
                if last_unit:
                    pe.wait_ge(lo_dve, N_DVE_LO * NCHUNK + on_pool(k))
                elif on_pool(k):
                    pe.wait_ge(lo_pool, N_POOL_LO * c + lo_count(k))
                else:
                    pe.wait_ge(lo_dve, N_DVE_LO * c + lo_count(k))
                if b == 0 and first and e == 1:
                    pe.wait_ge(warmed, 1)
                if b == 0 and not (first and e < 2):
                    pe.wait_ge(part_ready, E * c + e - 1)
                cols = slice(2 * F + b * D, 2 * F + (b + 1) * D)
                last = exact(y_ps[e % 2][:], w_hi[:, e, cols], w_lo[:, e, cols],
                             hid_hi[:, k % RING, :], hid_lo[:, k % RING, :], start=b == 0, stop=b == NB - 1)
                last.then_inc(down_done, 1)

            pe.wait_ge(angle_loaded, 32)
            nc.tensor.matmul(m_ps[:, 0:1], sines[:], a_col[:], start=True, stop=True).then_inc(omega_ready, 1)
            pe.wait_ge(const_ready, 4)
            keep_warm(WARM[0])
            turn_tiles(0).then_inc(xn_turned, 1)
            keep_warm(WARM[1])
            pe.wait_ge(proj_split, 2)
            mix_bu(0, prologue=True)
            keep_warm(WARM[2])
            mix_c(0)
            mix_turn_y(0, True)
            keep_warm(WARM[3])
            turn_tiles(1).then_inc(xe_turned, 1)
            keep_warm(WARM[4]).then_inc(warmed, 1)
            pe.wait_ge(xe_hi_ready, 1)
            pe.wait_ge(xe_lo_ready, 1)

            def body(c, par, first, last):
                for k in range(UNITS):
                    gate_up(c, par, k, first)
                    if k >= LAG:
                        down(c, k - LAG, first)
                    elif not first:
                        down(c - 1, k - LAG + UNITS, False)
                    if first and k == 0:
                        mix_logits(0, 0)
                    if k == (4 if first else TENSOR_AT["turn_cw"]):
                        mix_turn_cw(c)
                    if not last:
                        if k == TENSOR_AT["turn_x"]:
                            mix_turn_x(c + 1)
                        if k == TENSOR_AT["bu"]:
                            mix_bu(c + 1)
                        if k == TENSOR_AT["c"]:
                            mix_c(c + 1)
                        if k == TENSOR_AT["turn_y"]:
                            mix_turn_y(c + 1, first)
                        if k == TENSOR_AT["turn_xe"]:
                            mix_turn_xe(c + 1)
                        if k == TENSOR_AT["logits"]:
                            mix_logits(c + 1, 1 - par)
                    if k == TENSOR_AT["turn_out"] and not first:
                        turn_out(c - 1, 1 - par, tail=last)

            for_chunks(pe, body)
            for k in range(UNITS - LAG, UNITS):
                down(NCHUNK - 1, k, False, last_unit=k == UNITS - 1)
            turn_out(NCHUNK - 1, (NCHUNK - 1) % 2, last=True)

        @block.scalar
        def _(act):
            def round_piece(e, i):
                if i == 0:
                    act.wait_ge(w_loaded[e % 2], 48 * (e // 2 + 1))
                cols = slice(i * F, (i + 1) * F)
                nc.scalar.activation(w_hi[:, e, cols], stage[:, e % 2, cols], ACT.Copy).then_inc(w_hi_done, 1)

            def mix_hi_x(c):
                act.wait_ge(xn_turned, c + 1)
                nc.scalar.activation(act_hi[:], n_ps[:], ACT.Copy).then_inc(act_hi_ready, 1)

            def mix_du(c):
                nc.scalar.activation(y_sb[:], n_ps[:], ACT.Copy, scale=d_col[:]).then_inc(du_ready, 1)

            def mix_hi_w(c):
                act.wait_ge(w_ready, c + 1)
                nc.scalar.activation(act_hi[:], v_sb[:], ACT.Copy).then_inc(act_hi_ready, 1)

            def mix_z(c, tiles):
                if tiles[0] == 0:
                    act.wait_ge(shift_ready, c + 1)
                for j in tiles:
                    last = nc.scalar.activation(z_sb[:, j, :], n_ps[:, j * P:(j + 1) * P], ACT.Identity,
                                                bias=shift[:, j:j + 1], scale=rstd[:, j:j + 1])
                if tiles[-1] == NT - 1:
                    last.then_inc(z_ready, 1)

            def mix_hi_xe(c, par):
                act.wait_ge(xe_turned, c + 1)
                nc.scalar.activation(xe_hi[:, par, :], n_ps[:], ACT.Copy).then_inc(xe_hi_ready, 1)

            def mix_silus(c):
                act.wait_ge(lg_ready, c + 1)
                nc.scalar.activation(e_neg[:], lg[:], ACT.Silu, bias=-1.0)
                nc.scalar.activation(e_pos[:], lg[:], ACT.Silu, bias=1.0, scale=-1.0).then_inc(silus_ready, 1)

            def mix_cw_t(c, first):
                act.wait_ge(cw_turned, c + 1)
                if not first:
                    act.wait_ge(cw_stored, 16 * c)
                nc.scalar.activation(cw_t[:], n_ps[0:E * NT, 0:P], ACT.Copy).then_inc(cw_t_ready, 1)

            def fin_scale(c, tiles):
                if tiles[0] == 0:
                    act.wait_ge(fin_shift, c + 1)
                    act.wait_ge(out_free, 16 * (c + 1))
                for j in tiles:
                    last = nc.scalar.activation(o_sb[:, j, :], n_ps[:, j * P:(j + 1) * P], ACT.Identity,
                                                bias=shift2[:, j:j + 1], scale=rstd2[:, j:j + 1])
                if tiles[-1] == NT - 1:
                    last.then_inc(fin_z, 1)

            def silu(c, k, first):
                act.wait_ge(g_done, UNITS * c + k + 1)
                if not (first and k < 2):
                    act.wait_ge(hid_ready, UNITS * c + k - 1)
                nc.scalar.activation(gate[:, k % 2, :], g_ps[k % 2][:], ACT.Silu).then_inc(gate_ready, 1)

            def hid_high(c, k, first):
                act.wait_ge(hid_ready, UNITS * c + k + 1)
                if not (first and k < RING):
                    act.wait_ge(down_done, UNITS * c + k + 1 - RING)
                nc.scalar.activation(hid_hi[:, k % RING, :], hid[:, k % RING, :], ACT.Copy).then_inc(hi_ready, 1)

            act.wait_ge(const_ready, 4)
            nc.scalar.activation(ang[:, 6:7], ident[:, 0:1], ACT.Silu)
            act.wait_ge(small_loaded, 32)
            nc.scalar.activation(router[:, 0, :], proj[:, P + D:], ACT.Copy)
            nc.scalar.activation(proj_hi[:], proj[:, 0:P + D], ACT.Copy).then_inc(proj_split, 1)
            mix_hi_x(0)
            mix_du(0)
            for n in range(2 * PIECES):
                round_piece(n // PIECES, n % PIECES)
            act.wait_ge(w_half, 1)
            nc.scalar.activation(act_hi[:, 0:HALF], v_sb[:, 0:HALF], ACT.Copy).then_inc(act_hi_half, 1)
            act.wait_ge(w_ready, 1)
            nc.scalar.activation(act_hi[:, HALF:], v_sb[:, HALF:], ACT.Copy).then_inc(act_hi_ready, 1)
            for n in range(2 * PIECES, AHEAD * PIECES):
                round_piece(n // PIECES, n % PIECES)
            act.wait_ge(shift_ready, 1)
            for j in range(NT):
                nc.scalar.activation(z_sb[:, j, :], n_ps[:, j * P:(j + 1) * P], ACT.Identity, bias=shift[:, j:j + 1],
                                     scale=rstd[:, j:j + 1]).then_inc(z_tile if j < NT - 1 else z_ready, 1)
            mix_hi_xe(0, 0)

            def body(c, par, first, last):
                for k in range(UNITS):
                    silu(c, k, first)
                    if k >= 1:
                        hid_high(c, k - 1, first)
                    elif not first:
                        hid_high(c - 1, UNITS - 1, False)
                    if first and k % 2 == 1 and k // 2 < (E - AHEAD) * PIECES:
                        round_piece(AHEAD + k // 2 // PIECES, k // 2 % PIECES)
                    if first and k == 1:
                        mix_silus(0)
                    if k == (4 if first else SCALAR_AT["cw_t"]):
                        mix_cw_t(c, first)
                    if not last:
                        if k == SCALAR_AT["hi_x"]:
                            mix_hi_x(c + 1)
                        if k == SCALAR_AT["du"]:
                            mix_du(c + 1)
                        if k == SCALAR_AT["hi_w"]:
                            mix_hi_w(c + 1)
                        if k == SCALAR_AT["z_a"]:
                            mix_z(c + 1, (0, 1))
                        if k == SCALAR_AT["z_b"]:
                            mix_z(c + 1, (2, 3))
                        if k == SCALAR_AT["hi_xe"]:
                            mix_hi_xe(c + 1, 1 - par)
                        if k == SCALAR_AT["silus"]:
                            mix_silus(c + 1)
                    if not first:
                        if k == SCALAR_AT["fin_a"]:
                            fin_scale(c - 1, (0, 1))
                        if k == SCALAR_AT["fin_b"]:
                            fin_scale(c - 1, (2, 3))

            for_chunks(act, body)
            hid_high(NCHUNK - 1, UNITS - 1, False)
            act.wait_ge(fin_shift, NCHUNK)
            act.wait_ge(out_free, 16 * NCHUNK)
            for j in range(NT):
                nc.scalar.activation(o_sb[:, j, :], n_ps[:, j * P:(j + 1) * P], ACT.Identity, bias=shift2[:, j:j + 1],
                                     scale=rstd2[:, j:j + 1]).then_inc(fin_tile if j < NT - 1 else fin_z, 1)

        @block.vector
        def _(dve):
            def measure(src, st, link):
                for j in range(NT):
                    last = nc.vector.bn_stats(st[:, j, :], src(j))
                last.then_inc(link, 1)

            def mean_var_1(st, m, ve, link, at):
                dve.wait_ge(link, at + 1)
                nc.vector.tensor_tensor(m[:], st[:, :, 1:3], st[:, :, 4:6], ALU.add)
                nc.vector.tensor_tensor(ve[:], st[:, :, 1], st[:, :, 4], ALU.subtract).then_inc(link, 1)

            def mean_var_2(m, ve, link, at):
                dve.wait_ge(link, at + 2)
                nc.vector.tensor_tensor(m[:], m[:], pair_mean[:], ALU.mult)
                nc.vector.scalar_tensor_tensor(out=ve[:], in0=ve[:], scalar=0.25, in1=ve[:], op0=ALU.mult,
                                               op1=ALU.mult).then_inc(link, 1)

            def mean_var_3(m, ve, link, at):
                dve.wait_ge(link, at + 3)
                return nc.vector.scalar_tensor_tensor(out=ve[:], in0=m[:, :, 1], scalar=LN_EPS, in1=ve[:],
                                                      op0=ALU.add, op1=ALU.add)

            def mean_var(st, m, ve, link, at):
                mean_var_1(st, m, ve, link, at)
                mean_var_2(m, ve, link, at)
                return mean_var_3(m, ve, link, at)

            def normalise(dst, src):
                for j in range(NT):
                    last = nc.vector.tensor_scalar(dst[:, j, :], src(j), mv[:, j, 0:1], rstd[:, j:j + 1],
                                                   ALU.subtract, ALU.mult)
                return last

            def shifts(dst, m, r):
                return nc.vector.scalar_tensor_tensor(out=dst[:], in0=m[:, :, 0], scalar=-1.0, in1=r[:],
                                                      op0=ALU.mult, op1=ALU.mult)

            def mix_stats_x(c):
                dve.wait_ge(x_loaded, 16 * (c + 1))
                measure(lambda j: x_sb[:, j, :], stats, mix_link)

            def mix_var(c, n):
                at = MIX_LINKS * c + (0, 5, 8)[n - 1]
                mean_var(stats, mv, var_eps, mix_link, at).then_inc(var_ready, 1)

            def mix_norm_x(c):
                dve.wait_ge(rstd_ready, 3 * c + 1)
                normalise(xn, lambda j: x_sb[:, j, :]).then_inc(xn_ready, 1)

            def mix_lo_x(c):
                dve.wait_ge(du_ready, c + 1)
                nc.vector.tensor_tensor(act_lo[:], n_ps[:], act_hi[:].bitcast(f32), ALU.subtract).then_inc(act_lo_ready, 1)

            def mix_enter(c):
                dve.wait_ge(bu_ready, c + 1)
                nc.vector.tensor_tensor(v_sb[:], m_ps[:], trig[:], ALU.mult).then_inc(mix_link, 1)

            def mix_scan(c):
                dve.wait_ge(mix_link, MIX_LINKS * c + 4)
                nc.vector.tensor_tensor_scan(sum_sb[:], v_sb[:], v_sb[:], 0.0, ALU.add, ALU.bypass).then_inc(mix_link, 1)

            def mix_leave(c):
                dve.wait_ge(mix_link, MIX_LINKS * c + 5)
                nc.vector.tensor_tensor(v_sb[:], sum_sb[:], trig[:], ALU.mult).then_inc(w_ready, 1)

            def mix_lo_w(c):
                dve.wait_ge(w_ready, c + 1)
                dve.wait_ge(act_hi_ready, 2 * c + 2)
                nc.vector.tensor_tensor(act_lo[:], v_sb[:], act_hi[:].bitcast(f32), ALU.subtract).then_inc(act_lo_ready, 1)

            def mix_y(c):
                dve.wait_ge(mixed_ready, c + 1)
                nc.vector.tensor_tensor(y_sb[:], m_ps[:], y_sb[:], ALU.add).then_inc(y_ready, 1)

            def mix_stats_y(c):
                dve.wait_ge(y_turned, c + 1)
                measure(lambda j: n_ps[:, j * P:(j + 1) * P], stats, mix_link)

            def mix_shift(c):
                dve.wait_ge(rstd_ready, 3 * c + 2)
                shifts(shift, mv, rstd).then_inc(shift_ready, 1)

            def mix_stats_x1(c, par):
                dve.wait_ge(x1_ready, c + 1)
                measure(lambda j: x1[:, par, j, :], stats, mix_link)

            def mix_norm_x1(c, par):
                dve.wait_ge(rstd_ready, 3 * c + 3)
                normalise(xn, lambda j: x1[:, par, j, :]).then_inc(xn_ready, 1)

            def mix_lo_xe(c, par):
                dve.wait_ge(xe_hi_ready, c + 1)
                nc.vector.tensor_tensor(xe_lo[:, par, :], n_ps[:], xe_hi[:, par, :].bitcast(f32), ALU.subtract).then_inc(xe_lo_ready, 1)

            def groups(t):
                return t[:].rearrange("p j r e -> p (j r) e")

            def wide(t, n):
                return t.unsqueeze(2).broadcast_to([P, t.shape[1], n])

            def mix_softmax_in(c):
                at = SOFT_LINKS * c
                pair = "p j r -> p (j r)"
                dve.wait_ge(logits_ready, c + 1)
                nc.vector.tensor_reduce(out=lg[:].rearrange("p j r e -> p j (r e)"),
                                        in_=m_ps[:, 0:NT * 4 * E].rearrange("p (j h q) -> p j q h", j=NT, h=2),
                                        op=ALU.add, axis=AX.X).then_inc(raw_read, 1)
                dve.wait_ge(raw_read, c + 1)
                nc.vector.tensor_reduce(out=gmax[:].rearrange(pair), in_=groups(lg), op=ALU.max,
                                        axis=AX.X).then_inc(soft_link, 1)
                dve.wait_ge(soft_link, at + 1)
                nc.vector.tensor_tensor(groups(lg), groups(lg), wide(gmax[:].rearrange(pair), E),
                                        ALU.subtract).then_inc(soft_link, 1)
                dve.wait_ge(soft_link, at + 2)
                nc.vector.tensor_tensor(lg[:], lg[:], sharp[:], ALU.mult).then_inc(lg_ready, 1)

            def mix_exps(c):
                at = SOFT_LINKS * c + 2
                dve.wait_ge(silus_ready, c + 1)
                nc.vector.reciprocal(e_pos[:], e_pos[:]).then_inc(soft_link, 1)
                dve.wait_ge(soft_link, at + 1)
                nc.vector.scalar_tensor_tensor(out=groups(lg), in0=groups(e_neg), scalar=-1.0, in1=groups(e_pos),
                                               op0=ALU.mult, op1=ALU.mult).then_inc(soft_link, 1)

            def mix_products(c):
                at = SOFT_LINKS * c + 4
                dve.wait_ge(soft_link, at)
                nc.vector.tensor_tensor(pr[:], lg[:, :, 0, :], lg[:, :, 1, :], ALU.mult)
                nc.vector.tensor_reduce(out=gsum[:].rearrange("p j r -> p (j r)"), in_=groups(lg), op=ALU.add,
                                        axis=AX.X).then_inc(soft_link, 1)
                dve.wait_ge(soft_link, at + 1)
                nc.vector.tensor_reduce(out=psum_[:], in_=pr[:], op=ALU.add, axis=AX.X)
                nc.vector.tensor_tensor(den[:], gsum[:, :, 0], gsum[:, :, 1], ALU.mult).then_inc(soft_link, 1)

            def mix_weights(c):
                at = SOFT_LINKS * c + 6
                dve.wait_ge(soft_link, at)
                nc.vector.scalar_tensor_tensor(out=den[:], in0=den[:], scalar=MIX_EPS, in1=psum_[:],
                                               op0=ALU.mult, op1=ALU.add).then_inc(soft_link, 1)
                dve.wait_ge(soft_link, at + 1)
                nc.vector.reciprocal(den[:], den[:]).then_inc(soft_link, 1)
                dve.wait_ge(soft_link, at + 2)
                nc.vector.tensor_tensor(cw_pad[:, 0:E * NT].rearrange("p (e j) -> p j e", j=NT), pr[:],
                                        wide(den[:], E), ALU.mult).then_inc(cw_ready, 1)

            def fin_stats(c):
                dve.wait_ge(fin_turned, c + 1)
                measure(lambda j: n_ps[:, j * P:(j + 1) * P], stats2, fin_link)

            def fin_mean_var(c):
                mean_var(stats2, mv2, var_eps2, fin_link, FIN_LINKS * c).then_inc(fin_var, 1)

            def fin_shifts(c):
                dve.wait_ge(fin_rstd, c + 1)
                shifts(shift2, mv2, rstd2).then_inc(fin_shift, 1)

            def hidden(c, k, first):
                dve.wait_ge(gate_ready, UNITS * c + k + 1)
                dve.wait_ge(u_done, UNITS * c + k + 1)
                if not (first and k < RING):
                    cc, kk = (c, k - RING) if k >= RING else (c - 1, k - RING + UNITS)
                    if on_pool(kk):
                        dve.wait_ge(lo_pool, N_POOL_LO * cc + lo_count(kk))
                    else:
                        dve.wait_ge(lo_dve, N_DVE_LO * cc + lo_count(kk))
                nc.vector.tensor_tensor(hid[:, k % RING, :], gate[:, k % 2, :], u_ps[k % 2][:], ALU.mult).then_inc(hid_ready, 1)

            def hid_low(c, k, first, last_unit=False):
                if on_pool(k) and not last_unit:
                    return
                dve.wait_ge(hi_ready, UNITS * c + k + 1)
                nc.vector.tensor_tensor(hid_lo[:, k % RING, :], hid[:, k % RING, :], hid_hi[:, k % RING, :].bitcast(f32),
                                        ALU.subtract).then_inc(lo_dve, 1)

            def weigh(c, par, e, first):
                dve.wait_ge(down_done, UNITS * c + NB * (e + 1))
                dve.wait_ge(cw_spread[e % 4], 16 * (2 * c + e // 4 + 1))
                if e > 0 and not (first and e < 3):
                    dve.wait_ge(part_added, ADDS * c + max(e - 2, 0))
                dst = acc[:, par, :] if e == 0 else y_part[:, e % 2, :]
                nc.vector.tensor_tensor(dst, y_ps[e % 2][:], cw_b[:, e % 4, :], ALU.mult).then_inc(part_ready, 1)

            links = [0]

            def then(ins, *meanwhile):
                links[0] += 1
                ins.then_inc(trig_link, 1)
                for step in meanwhile:
                    step()
                dve.wait_ge(trig_link, links[0])

            w, w2, r, norm = (ang[:, i:i + 1] for i in range(4))
            nc.vector.memset(half[:], -0.5).then_inc(out_free, 16)
            nc.vector.memset(pair_mean[:, :, 0], 0.5)
            nc.vector.memset(pair_mean[:, :, 1], 1.0 / D)
            nc.vector.memset(sharp[:, :, 0, :], 1.0)
            nc.vector.memset(sharp[:, :, 1, :], GATE_SHARP)
            nc.vector.memset(cw_pad[:], 0.0).then_inc(const_ready, 1)
            slope = sum_sb
            v_cos, v_sin = v_sb, z_sb[:].rearrange("p j d -> p (j d)")
            nc.vector.memset(low[:, 0, 0:1], 1.0)
            nc.vector.memset(low[:, 1, 0:1], 0.0)
            dve.wait_ge(const_ready, 2)
            dve.wait_ge(omega_ready, 1)
            co, si = low[:, 0, 1:2], low[:, 1, 1:2]
            then(nc.vector.tensor_copy(w, m_ps[:, 0:1]))
            then(nc.vector.tensor_tensor(w2, w, w, ALU.mult))
            nc.vector.tensor_scalar(co, w2, -1.0, 1.0, ALU.mult, ALU.add)
            then(nc.vector.tensor_scalar(r, w2, 1.0, None, ALU.add))
            then(nc.vector.reciprocal(r, r))
            nc.vector.scalar_tensor_tensor(out=si, in0=w, scalar=-2.0, in1=r, op0=ALU.mult, op1=ALU.mult)
            then(nc.vector.tensor_tensor(co, co, r, ALU.mult), lambda: mix_stats_x(0))

            def unit(n, *meanwhile):
                co, si = low[:, 0, n:n + 1], low[:, 1, n:n + 1]
                then(nc.vector.tensor_tensor(norm, si, si, ALU.mult), *meanwhile[0:1])
                then(nc.vector.scalar_tensor_tensor(out=norm, in0=co, scalar=co, in1=norm, op0=ALU.mult,
                                                    op1=ALU.add), *meanwhile[1:2])
                then(nc.vector.tensor_scalar(norm, norm, -0.5, 1.5, ALU.mult, ALU.add), *meanwhile[2:3])
                then(nc.vector.tensor_scalar(low[:, :, n:n + 1], low[:, :, n:n + 1], norm, None, ALU.mult))

            unit(1, lambda: mean_var_1(stats, mv, var_eps, mix_link, 0), lambda: mean_var_2(mv, var_eps, mix_link, 0),
                 lambda: mean_var_3(mv, var_eps, mix_link, 0).then_inc(var_ready, 1))
            n = 1
            while n < SMALL:
                if n == 4:
                    unit(4)
                co, si = low[:, 0, n:n + 1], low[:, 1, n:n + 1]
                old, new = slice(1, n + 1), slice(n + 1, 2 * n + 1)
                nc.vector.tensor_scalar(v_cos[:, old], low[:, 1, old], si, None, ALU.mult)
                then(nc.vector.tensor_scalar(v_sin[:, old], low[:, 0, old], si, None, ALU.mult))
                nc.vector.scalar_tensor_tensor(out=low[:, 0, new], in0=low[:, 0, old], scalar=co, in1=v_cos[:, old],
                                               op0=ALU.mult, op1=ALU.subtract)
                then(nc.vector.scalar_tensor_tensor(out=low[:, 1, new], in0=low[:, 1, old], scalar=co,
                                                    in1=v_sin[:, old], op0=ALU.mult, op1=ALU.add))
                n *= 2
            nc.vector.tensor_copy(trig[0:NS, 0:n], low[0:NS, 0, 0:n])
            nc.vector.tensor_copy(trig[NS:P, 0:n], low[NS:P, 1, 0:n])
            nc.vector.tensor_scalar(slope[0:NS, 0:n], low[0:NS, 1, 0:n], -1.0, None, ALU.mult)
            then(nc.vector.tensor_copy(slope[NS:P, 0:n], low[NS:P, 0, 0:n]))
            co, si = low[:, 0, n:n + 1], low[:, 1, n:n + 1]
            level = 0
            while n < SEQ:
                old, new = slice(0, n), slice(n, 2 * n)
                if n == SEQ // 2:
                    then(nc.vector.tensor_scalar(v_cos[:, old], slope[:, old], si, None, ALU.mult))
                    nc.vector.scalar_tensor_tensor(out=trig[:, new], in0=trig[:, old], scalar=co, in1=v_cos[:, old],
                                                   op0=ALU.mult, op1=ALU.add).then_inc(trig_ready, 1)
                    break
                co2, si2 = high[:, 0, level:level + 1], high[:, 1, level:level + 1]
                nc.vector.tensor_tensor(norm, si, si, ALU.mult)
                nc.vector.scalar_tensor_tensor(out=si2, in0=si, scalar=2.0, in1=co, op0=ALU.mult, op1=ALU.mult)
                nc.vector.tensor_scalar(v_cos[:, old], slope[:, old], si, None, ALU.mult)
                then(nc.vector.tensor_scalar(v_sin[:, old], trig[:, old], si, None, ALU.mult))
                nc.vector.scalar_tensor_tensor(out=co2, in0=co, scalar=co, in1=norm, op0=ALU.mult, op1=ALU.subtract)
                nc.vector.scalar_tensor_tensor(out=trig[:, new], in0=trig[:, old], scalar=co, in1=v_cos[:, old],
                                               op0=ALU.mult, op1=ALU.add)
                then(nc.vector.scalar_tensor_tensor(out=slope[:, new], in0=slope[:, old], scalar=co,
                                                    in1=v_sin[:, old], op0=ALU.mult, op1=ALU.subtract))
                co, si = co2, si2
                if n == 2 * SMALL:
                    mix_lo_x(0)
                level += 1
                n *= 2
            dve.wait_ge(trig_ready, 1)
            mix_enter(0)
            mix_scan(0)
            dve.wait_ge(mix_link, 5)
            nc.vector.tensor_tensor(v_sb[:, 0:HALF], sum_sb[:, 0:HALF], trig[:, 0:HALF], ALU.mult).then_inc(w_half, 1)
            nc.vector.tensor_tensor(v_sb[:, HALF:], sum_sb[:, HALF:], trig[:, HALF:], ALU.mult).then_inc(w_ready, 1)
            dve.wait_ge(w_half, 1)
            dve.wait_ge(act_hi_half, 1)
            nc.vector.tensor_tensor(act_lo[:, 0:HALF], v_sb[:, 0:HALF], act_hi[:, 0:HALF].bitcast(f32), ALU.subtract)
            dve.wait_ge(w_ready, 1)
            dve.wait_ge(act_hi_ready, 2)
            nc.vector.tensor_tensor(act_lo[:, HALF:], v_sb[:, HALF:], act_hi[:, HALF:].bitcast(f32),
                                    ALU.subtract).then_inc(act_lo_ready, 1)
            mix_y(0)
            mix_stats_y(0)
            mix_var(0, 2)
            mix_shift(0)
            for j in range(NT + 1):
                if j < NT:
                    if j < NT - 1:
                        dve.wait_ge(z_tile, j + 1)
                    else:
                        dve.wait_ge(z_ready, 1)
                    nc.vector.tensor_tensor(x1[:, 0, j, :], x_sb[:, j, :], z_sb[:, j, :],
                                            ALU.add).then_inc(x1_tile if j < NT - 1 else x1_ready, 1)
                if j > 0:
                    if j < NT:
                        dve.wait_ge(x1_tile, j)
                    else:
                        dve.wait_ge(x1_ready, 1)
                    last = nc.vector.bn_stats(stats[:, j - 1, :], x1[:, 0, j - 1, :])
            last.then_inc(mix_link, 1)
            mix_var(0, 3)
            dve.wait_ge(rstd_ready, 3)
            for j in range(NT):
                nc.vector.tensor_scalar(xn[:, j, :], x1[:, 0, j, :], mv[:, j, 0:1], rstd[:, j:j + 1], ALU.subtract,
                                        ALU.mult).then_inc(xn_tile if j < NT - 1 else xn_ready, 1)
            mix_lo_xe(0, 0)

            def body(c, par, first, last):
                for k in range(UNITS):
                    hidden(c, k, first)
                    if k >= 1:
                        hid_low(c, k - 1, first)
                    elif not first:
                        hid_low(c - 1, UNITS - 1, False)
                    if first and k == 0:
                        mix_softmax_in(0)
                    if first and k == 1:
                        mix_exps(0)
                        mix_products(0)
                    if k == (2 if first else VECTOR_AT["weights"]):
                        mix_weights(c)
                    if k % NB == 0 and k >= 8:
                        weigh(c, par, k // NB - 2, first)
                    if k in (0, 4) and not first:
                        weigh(c - 1, 1 - par, E - 2 + k // NB, False)
                    if not last:
                        if k == VECTOR_AT["stats_x"]:
                            mix_stats_x(c + 1)
                        if k == VECTOR_AT["var_x"]:
                            mix_var(c + 1, 1)
                        if k == VECTOR_AT["norm_x"]:
                            mix_norm_x(c + 1)
                        if k == VECTOR_AT["lo_x"]:
                            mix_lo_x(c + 1)
                        if k == VECTOR_AT["enter"]:
                            mix_enter(c + 1)
                        if k == VECTOR_AT["scan"]:
                            mix_scan(c + 1)
                        if k == VECTOR_AT["leave"]:
                            mix_leave(c + 1)
                        if k == VECTOR_AT["lo_w"]:
                            mix_lo_w(c + 1)
                        if k == VECTOR_AT["y"]:
                            mix_y(c + 1)
                        if k == VECTOR_AT["stats_y"]:
                            mix_stats_y(c + 1)
                        if k == VECTOR_AT["var_y"]:
                            mix_var(c + 1, 2)
                        if k == VECTOR_AT["shift"]:
                            mix_shift(c + 1)
                        if k == VECTOR_AT["stats_x1"]:
                            mix_stats_x1(c + 1, 1 - par)
                        if k == VECTOR_AT["var_x1"]:
                            mix_var(c + 1, 3)
                        if k == VECTOR_AT["norm_x1"]:
                            mix_norm_x1(c + 1, 1 - par)
                        if k == VECTOR_AT["lo_xe"]:
                            mix_lo_xe(c + 1, 1 - par)
                        if k == VECTOR_AT["softmax"]:
                            mix_softmax_in(c + 1)
                        if k == VECTOR_AT["exps"]:
                            mix_exps(c + 1)
                        if k == VECTOR_AT["products"]:
                            mix_products(c + 1)
                    if not first:
                        if k == VECTOR_AT["fin_stats"]:
                            fin_stats(c - 1)
                        if k == VECTOR_AT["fin_var"]:
                            fin_mean_var(c - 1)
                        if k == VECTOR_AT["fin_shift"]:
                            fin_shifts(c - 1)

            for_chunks(dve, body)
            hid_low(NCHUNK - 1, UNITS - 1, False, last_unit=True)
            weigh(NCHUNK - 1, (NCHUNK - 1) % 2, E - 2, False)
            weigh(NCHUNK - 1, (NCHUNK - 1) % 2, E - 1, False)
            dve.wait_ge(part_ready, E * NCHUNK)
            dve.wait_ge(part_added, ADDS * NCHUNK - 1)
            end = (NCHUNK - 1) % 2
            nc.vector.tensor_tensor(acc[:, end, :], acc[:, end, :], y_part[:, (E - 1) % 2, :],
                                    ALU.add).then_inc(part_added, 1)
            fin_stats(NCHUNK - 1)
            fin_mean_var(NCHUNK - 1)
            fin_shifts(NCHUNK - 1)
            for j in range(NT):
                if j < NT - 1:
                    dve.wait_ge(fin_tile, j + 1)
                else:
                    dve.wait_ge(fin_z, NCHUNK)
                last = nc.vector.tensor_tensor(o_sb[:, j, :], x1[:, end, j, :], o_sb[:, j, :], ALU.add)
            last.then_inc(fin_ready, 1)

        @block.gpsimd
        def _(pool):
            def split_piece(e, i):
                pool.wait_ge(w_hi_done, PIECES * e + i + 1)
                cols = slice(i * F, (i + 1) * F)
                nc.gpsimd.tensor_tensor(w_lo[:, e, cols], stage[:, e % 2, cols], w_hi[:, e, cols].bitcast(f32),
                                        ALU.subtract).then_inc(w_lo_done, 1)

            def mix_rstd(c, n):
                pool.wait_ge(var_ready, 3 * c + n)
                nc.gpsimd.tensor_tensor(rstd[:], var_eps[:], half[:], ALU.pow).then_inc(rstd_ready, 1)

            def mix_residual(c, par):
                pool.wait_ge(z_ready, c + 1)
                nc.gpsimd.tensor_tensor(x1[:, par], x_sb[:], z_sb[:], ALU.add).then_inc(x1_ready, 1)

            def fin_rsqrt(c):
                pool.wait_ge(fin_var, c + 1)
                nc.gpsimd.tensor_tensor(rstd2[:], var_eps2[:], half[:], ALU.pow).then_inc(fin_rstd, 1)

            def fin_residual(c, par):
                pool.wait_ge(fin_z, c + 1)
                nc.gpsimd.tensor_tensor(o_sb[:], x1[:, par], o_sb[:], ALU.add).then_inc(fin_ready, 1)

            def hid_low(c, k, first):
                if not on_pool(k):
                    return
                pool.wait_ge(hi_ready, UNITS * c + k + 1)
                nc.gpsimd.tensor_tensor(hid_lo[:, k % RING, :], hid[:, k % RING, :], hid_hi[:, k % RING, :].bitcast(f32),
                                        ALU.subtract).then_inc(lo_pool, 1)

            def add_part(c, par, e):
                pool.wait_ge(part_ready, E * c + e + 1)
                if e > 1:
                    pool.wait_ge(part_added, ADDS * c + e - 1)
                nc.gpsimd.tensor_tensor(acc[:, par, :], acc[:, par, :], y_part[:, e % 2, :], ALU.add).then_inc(part_added, 1)

            nc.gpsimd.memset(ident[:], 0.0).then_inc(const_ready, 1)
            pool.wait_ge(const_ready, 2)
            nc.gpsimd.affine_select(out=ident[:], in_=ident[:], compare_op=ALU.not_equal, fill=1.0, base=0,
                                    pattern=[[-1, P]], channel_multiplier=1).then_inc(const_ready, 2)
            mix_rstd(0, 1)
            pool.wait_ge(rstd_ready, 1)
            for j in range(NT):
                nc.gpsimd.tensor_scalar(xn[:, j, :], x_sb[:, j, :], mv[:, j, 0:1], rstd[:, j:j + 1], ALU.subtract,
                                        ALU.mult).then_inc(xn_tile if j < NT - 1 else xn_ready, 1)
            pool.wait_ge(proj_split, 1)
            nc.gpsimd.tensor_tensor(router[:, 1, :], proj[:, P + D:], router[:, 0, :].bitcast(f32), ALU.subtract)
            nc.gpsimd.tensor_tensor(proj_lo[:], proj[:, 0:P + D], proj_hi[:].bitcast(f32),
                                    ALU.subtract).then_inc(proj_split, 1)
            start = 0
            for norm, end in ((2, SPLIT_BEFORE[0]), (3, SPLIT_BEFORE[1]), (None, AHEAD * PIECES)):
                for n in range(start, end):
                    split_piece(n // PIECES, n % PIECES)
                if norm:
                    mix_rstd(0, norm)
                start = end

            def body(c, par, first, last):
                for k in range(UNITS):
                    if k >= 1:
                        hid_low(c, k - 1, first)
                    elif not first:
                        hid_low(c - 1, UNITS - 1, False)
                    if k % NB == 0 and k >= 12:
                        add_part(c, par, k // NB - 2)
                    if k in (0, 4) and not first:
                        add_part(c - 1, 1 - par, E - 2 + k // NB)
                    if first and k % 2 == 1 and k // 2 < (E - AHEAD) * PIECES:
                        split_piece(AHEAD + k // 2 // PIECES, k // 2 % PIECES)
                    if not last:
                        if k == GPSIMD_AT["rstd_x"]:
                            mix_rstd(c + 1, 1)
                        if k == GPSIMD_AT["rstd_y"]:
                            mix_rstd(c + 1, 2)
                        if k == GPSIMD_AT["residual"]:
                            mix_residual(c + 1, 1 - par)
                        if k == GPSIMD_AT["rstd_x1"]:
                            mix_rstd(c + 1, 3)
                    if not first:
                        if k == GPSIMD_AT["fin_rstd"]:
                            fin_rsqrt(c - 1)
                        if k == GPSIMD_AT["fin_add"]:
                            fin_residual(c - 1, 1 - par)

            for_chunks(pool, body)
            add_part(NCHUNK - 1, (NCHUNK - 1) % 2, E - 2)
            fin_rsqrt(NCHUNK - 1)


def sine_rows():
    m = np.arange(NS)
    source = np.where(m <= NS // 2, m - 1, NS - m)
    sign = np.where(m <= NS // 2, 1.0, -1.0) * (m > 0)
    wave = -np.sin(2.0 * np.pi * ((m[:, None] * m[None, :]) % NS) / NS)
    rows = np.zeros((NS // 2, NS))
    for i in range(1, NS):
        rows[source[i]] += sign[i] * wave[i]
    return np.concatenate([rows, rows], axis=1).astype(np.float32)


def kernel(L0_attn_u, L0_attn_a_params, L0_attn_B_w, L0_attn_C_w, L0_attn_D, L0_ffn_w_router, L0_ffn_w_gating,
           L0_ffn_w_gate, L0_ffn_w_up, L0_ffn_w_down):
    import concourse.bacc as bacc
    from concourse.bass_utils import run_bass_kernel_spmd

    b_t, c_t = np.asarray(L0_attn_B_w).T, np.asarray(L0_attn_C_w).T
    arrays = {
        "x_in": L0_attn_u,
        "proj_in": np.concatenate([b_t, b_t, np.concatenate([c_t, c_t], axis=0), L0_ffn_w_router, L0_ffn_w_gating], axis=1),
        "a_in": np.asarray(L0_attn_a_params).reshape(NS // 2, 1),
        "sines_in": sine_rows(),
        "d_in": np.asarray(L0_attn_D).reshape(D, 1),
        "wgate_in": L0_ffn_w_gate,
        "wup_in": L0_ffn_w_up,
        "wdown_in": L0_ffn_w_down,
    }
    arrays = {n: np.ascontiguousarray(a) for n, a in arrays.items()}
    nc = bacc.Bacc("TRN2", target_bir_lowering=False, num_devices=1)
    args = [nc.dram_tensor(n, a.shape, mybir.dt.from_np(a.dtype), kind="ExternalInput").ap() for n, a in arrays.items()]
    args.append(nc.dram_tensor("x_out", (NCHUNK, SEQ, D), mybir.dt.float32, kind="ExternalOutput").ap())
    build(nc, *args)
    return run_bass_kernel_spmd(nc, [arrays], core_ids=[0]).results[0]["x_out"]
```
